# Optimizing a Trainium2 kernel written in Bass

```python
import numpy as np
import jax
import jax.numpy as jnp

def _softmax(x, axis=-1):
    return jax.nn.softmax(x, axis=axis)

def _gelu(x):
    return jax.nn.gelu(x, approximate=True)

def _silu(x):
    return jax.nn.silu(x)

def _sigmoid(x):
    return jax.nn.sigmoid(x)

def _layernorm(x, axis=-1, eps=1e-05):
    m = jnp.mean(x, axis=axis, keepdims=True)
    v = jnp.var(x, axis=axis, keepdims=True)
    return (x - m) / jnp.sqrt(v + eps)

def _scatter_add(tgt, idx, src, axis=0):
    return tgt.at[idx].add(src)

def _segment_sum(src, seg, n):
    return jax.ops.segment_sum(src, seg, n)
kernel_name = 'mk_hybrid_d1_jaxref_r8_52dbc0'

def setup_inputs(seed: int=0):
    np.random.seed(seed)
    _w = jnp.asarray

    def _L0_attn_a_setup():
        import jax, jax.numpy as jnp
        import numpy as np
        DIM = 128
        N_HEADS = 16
        HEAD_DIM = DIM // N_HEADS
        WINDOW = 32
        STRIDE = 64
        PATTERN = 'combined'

        def _sparse_mask(T):
            rows = jnp.arange(T)[:, None]
            cols = jnp.arange(T)[None, :]
            causal = cols <= rows
            sliding = causal & (cols >= rows - WINDOW + 1)
            strided = causal & ((rows - cols) % STRIDE == 0)
            if PATTERN == 'sliding':
                return sliding
            if PATTERN == 'strided':
                return strided
            return sliding | strided
        key = jax.random.key(seed)
        kx, kq, kk, kv, ko = jax.random.split(key, 5)
        s = 1.0 / np.sqrt(DIM)
        return {'x': jax.random.normal(kx, (1, 512, DIM), dtype=jnp.float32), 'Wq': jax.random.normal(kq, (DIM, DIM), dtype=jnp.float32) * s, 'Wk': jax.random.normal(kk, (DIM, DIM), dtype=jnp.float32) * s, 'Wv': jax.random.normal(kv, (DIM, DIM), dtype=jnp.float32) * s, 'Wo': jax.random.normal(ko, (DIM, DIM), dtype=jnp.float32) * s}
    _L0_attn_a_in = _L0_attn_a_setup()

    def _L0_attn_b_setup():
        import jax, jax.numpy as jnp
        from jax import lax
        import numpy as np
        D_MODEL = 128
        D_STATE = 16
        D_CONV = 4
        EXPAND = 2
        D_INNER = EXPAND * D_MODEL
        DT_RANK = -(-D_MODEL // 16)
        BATCH, SEQLEN = (2, 128)

        def _mamba_block(x, ln_g, ln_b, W_in, conv_w, conv_b, W_xp, W_dt, b_dt, A_log, D_param, W_out, res_scale):
            B, L, D = x.shape
            E, N, K, R = (D_INNER, D_STATE, D_CONV, DT_RANK)
            mu = jnp.mean(x, axis=-1, keepdims=True)
            var = jnp.mean(jnp.square(x - mu), axis=-1, keepdims=True)
            xn = (x - mu) * lax.rsqrt(var + 1e-05) * ln_g + ln_b
            xz = jnp.einsum('bld,de->ble', xn, W_in)
            u, z = jnp.split(xz, 2, axis=-1)
            uc = u.transpose(0, 2, 1)
            conv = lax.conv_general_dilated(uc, conv_w[:, None, :], window_strides=(1,), padding=[(K - 1, 0)], feature_group_count=E, dimension_numbers=('NCH', 'OIH', 'NCH'))
            u2 = jax.nn.silu(conv + conv_b[None, :, None]).transpose(0, 2, 1)
            x_dbl = jnp.einsum('ble,er->blr', u2, W_xp)
            dt_lo, Bm, Cm = (x_dbl[..., :R], x_dbl[..., R:R + N], x_dbl[..., R + N:])
            dt = jax.nn.softplus(jnp.einsum('blr,re->ble', dt_lo, W_dt) + b_dt)
            A = -jnp.exp(A_log)

            def step(h, inp):
                dt_t, B_t, C_t, u_t = inp
                dA = jnp.exp(dt_t[..., None] * A)
                h = dA * h + (dt_t * u_t)[..., None] * B_t[:, None, :]
                y_t = jnp.einsum('ben,bn->be', h, C_t)
                return (h, y_t)
            h0 = jnp.zeros((B, E, N), x.dtype)
            xs = (dt.transpose(1, 0, 2), Bm.transpose(1, 0, 2), Cm.transpose(1, 0, 2), u2.transpose(1, 0, 2))
            _, ys = lax.scan(step, h0, xs)
            y = ys.transpose(1, 0, 2) + u2 * D_param
            y = y * jax.nn.silu(z)
            out = jnp.einsum('ble,ed->bld', y, W_out)
            return x + res_scale * out
        key = jax.random.key(seed)
        ks = jax.random.split(key, 12)
        s_in = 1.0 / np.sqrt(D_MODEL)
        s_e = 1.0 / np.sqrt(D_INNER)
        s_r = 1.0 / np.sqrt(DT_RANK)
        x = jax.random.normal(ks[0], (BATCH, SEQLEN, D_MODEL), jnp.float32)
        ln_g = jnp.ones((D_MODEL,), jnp.float32)
        ln_b = jnp.zeros((D_MODEL,), jnp.float32)
        W_in = jax.random.normal(ks[1], (D_MODEL, 2 * D_INNER), jnp.float32) * s_in
        conv_w = jax.random.normal(ks[2], (D_INNER, D_CONV), jnp.float32) * (1.0 / np.sqrt(D_CONV))
        conv_b = jnp.zeros((D_INNER,), jnp.float32)
        W_xp = jax.random.normal(ks[3], (D_INNER, DT_RANK + 2 * D_STATE), jnp.float32) * s_e
        W_dt = jax.random.normal(ks[4], (DT_RANK, D_INNER), jnp.float32) * s_r
        dt = jnp.exp(jax.random.uniform(ks[5], (D_INNER,)) * (np.log(0.1) - np.log(0.001)) + np.log(0.001))
        b_dt = dt + jnp.log(-jnp.expm1(-dt))
        A_log = jnp.log(jnp.broadcast_to(jnp.arange(1, D_STATE + 1, dtype=jnp.float32), (D_INNER, D_STATE)))
        D_param = jnp.ones((D_INNER,), jnp.float32)
        W_out = jax.random.normal(ks[6], (D_INNER, D_MODEL), jnp.float32) * s_e
        res_scale = jnp.ones((1,), jnp.float32)
        return dict(x=x, ln_g=ln_g, ln_b=ln_b, W_in=W_in, conv_w=conv_w, conv_b=conv_b, W_xp=W_xp, W_dt=W_dt, b_dt=b_dt, A_log=A_log, D_param=D_param, W_out=W_out, res_scale=res_scale)
    _L0_attn_b_in = _L0_attn_b_setup()

    def _L0_ffn_setup():
        import jax, jax.numpy as jnp
        import numpy as np
        import math
        D_IN = 128
        FEATURES = (512, 512, 128)
        BATCH, SEQ = (8, 256)

        def _conn_dense(kernel_bool, x):
            w = jnp.where(kernel_bool, jnp.float32(1.0), jnp.float32(-1.0))
            return x @ w
        key = jax.random.key(seed)
        kx, kk0, kk1, kk2 = jax.random.split(key, 4)
        x = jax.random.normal(kx, (BATCH, SEQ, D_IN), dtype=jnp.float32)
        k0 = jax.random.randint(kk0, (2 * D_IN, FEATURES[0]), 0, 2).astype(jnp.bool_)
        k1 = jax.random.randint(kk1, (FEATURES[0], FEATURES[1]), 0, 2).astype(jnp.bool_)
        k2 = jax.random.randint(kk2, (FEATURES[1], FEATURES[2]), 0, 2).astype(jnp.bool_)
        s0 = jnp.asarray(1.0 / math.sqrt(2 * D_IN), dtype=jnp.float32)
        s1 = jnp.asarray(1.0 / math.sqrt(FEATURES[0]), dtype=jnp.float32)
        s2 = jnp.asarray(1.0 / math.sqrt(FEATURES[1]), dtype=jnp.float32)
        return {'x': x, 'k0': k0, 'k1': k1, 'k2': k2, 's0': s0, 's1': s1, 's2': s2}
    _L0_ffn_in = _L0_ffn_setup()
    _d = {'L0_attn_a_x': _L0_attn_a_in['x'], 'L0_attn_a_Wq': _L0_attn_a_in['Wq'], 'L0_attn_a_Wk': _L0_attn_a_in['Wk'], 'L0_attn_a_Wv': _L0_attn_a_in['Wv'], 'L0_attn_a_Wo': _L0_attn_a_in['Wo'], 'L0_attn_b_ln_g': _L0_attn_b_in['ln_g'], 'L0_attn_b_ln_b': _L0_attn_b_in['ln_b'], 'L0_attn_b_W_in': _L0_attn_b_in['W_in'], 'L0_attn_b_conv_w': _L0_attn_b_in['conv_w'], 'L0_attn_b_conv_b': _L0_attn_b_in['conv_b'], 'L0_attn_b_W_xp': _L0_attn_b_in['W_xp'], 'L0_attn_b_W_dt': _L0_attn_b_in['W_dt'], 'L0_attn_b_b_dt': _L0_attn_b_in['b_dt'], 'L0_attn_b_A_log': _L0_attn_b_in['A_log'], 'L0_attn_b_D_param': _L0_attn_b_in['D_param'], 'L0_attn_b_W_out': _L0_attn_b_in['W_out'], 'L0_attn_b_res_scale': _L0_attn_b_in['res_scale'], 'L0_ffn_k0': _L0_ffn_in['k0'], 'L0_ffn_k1': _L0_ffn_in['k1'], 'L0_ffn_k2': _L0_ffn_in['k2'], 'L0_ffn_s0': _L0_ffn_in['s0'], 'L0_ffn_s1': _L0_ffn_in['s1'], 'L0_ffn_s2': _L0_ffn_in['s2']}
    _x0 = _d['L0_attn_a_x']
    _d['L0_attn_a_x'] = jax.random.normal(jax.random.fold_in(jax.random.key(seed), 1), (4, 1024, 128), dtype=_x0.dtype)
    del _x0
    return _d

def reference(L0_attn_a_x, L0_attn_a_Wq, L0_attn_a_Wk, L0_attn_a_Wv, L0_attn_a_Wo, L0_attn_b_ln_g, L0_attn_b_ln_b, L0_attn_b_W_in, L0_attn_b_conv_w, L0_attn_b_conv_b, L0_attn_b_W_xp, L0_attn_b_W_dt, L0_attn_b_b_dt, L0_attn_b_A_log, L0_attn_b_D_param, L0_attn_b_W_out, L0_attn_b_res_scale, L0_ffn_k0, L0_ffn_k1, L0_ffn_k2, L0_ffn_s0, L0_ffn_s1, L0_ffn_s2):

    def _L0_attn_a_ref(x, Wq, Wk, Wv, Wo):
        import jax, jax.numpy as jnp
        import numpy as np
        DIM = 128
        N_HEADS = 16
        HEAD_DIM = DIM // N_HEADS
        WINDOW = 32
        STRIDE = 64
        PATTERN = 'combined'

        def _sparse_mask(T):
            rows = jnp.arange(T)[:, None]
            cols = jnp.arange(T)[None, :]
            causal = cols <= rows
            sliding = causal & (cols >= rows - WINDOW + 1)
            strided = causal & ((rows - cols) % STRIDE == 0)
            if PATTERN == 'sliding':
                return sliding
            if PATTERN == 'strided':
                return strided
            return sliding | strided
        B, T, C = x.shape
        scale = HEAD_DIM ** (-0.5)

        def split_heads(t):
            return t.reshape(B, T, N_HEADS, HEAD_DIM).transpose(0, 2, 1, 3)
        Q = split_heads(jnp.einsum('btc,dc->btd', x, Wq))
        K = split_heads(jnp.einsum('btc,dc->btd', x, Wk))
        V = split_heads(jnp.einsum('btc,dc->btd', x, Wv))
        scores = jnp.einsum('bhqd,bhkd->bhqk', Q, K) * scale
        mask = _sparse_mask(T)
        scores = jnp.where(mask[None, None], scores, -jnp.inf)
        attn = jax.nn.softmax(scores, axis=-1)
        attn = jnp.nan_to_num(attn, nan=0.0)
        out = jnp.einsum('bhqk,bhkd->bhqd', attn, V)
        out = out.transpose(0, 2, 1, 3).reshape(B, T, C)
        return jnp.einsum('btc,dc->btd', out, Wo)

    def _L0_attn_b_ref(x, ln_g, ln_b, W_in, conv_w, conv_b, W_xp, W_dt, b_dt, A_log, D_param, W_out, res_scale):
        import jax, jax.numpy as jnp
        from jax import lax
        import numpy as np
        D_MODEL = 128
        D_STATE = 16
        D_CONV = 4
        EXPAND = 2
        D_INNER = EXPAND * D_MODEL
        DT_RANK = -(-D_MODEL // 16)
        BATCH, SEQLEN = (2, 128)

        def _mamba_block(x, ln_g, ln_b, W_in, conv_w, conv_b, W_xp, W_dt, b_dt, A_log, D_param, W_out, res_scale):
            B, L, D = x.shape
            E, N, K, R = (D_INNER, D_STATE, D_CONV, DT_RANK)
            mu = jnp.mean(x, axis=-1, keepdims=True)
            var = jnp.mean(jnp.square(x - mu), axis=-1, keepdims=True)
            xn = (x - mu) * lax.rsqrt(var + 1e-05) * ln_g + ln_b
            xz = jnp.einsum('bld,de->ble', xn, W_in)
            u, z = jnp.split(xz, 2, axis=-1)
            uc = u.transpose(0, 2, 1)
            conv = lax.conv_general_dilated(uc, conv_w[:, None, :], window_strides=(1,), padding=[(K - 1, 0)], feature_group_count=E, dimension_numbers=('NCH', 'OIH', 'NCH'))
            u2 = jax.nn.silu(conv + conv_b[None, :, None]).transpose(0, 2, 1)
            x_dbl = jnp.einsum('ble,er->blr', u2, W_xp)
            dt_lo, Bm, Cm = (x_dbl[..., :R], x_dbl[..., R:R + N], x_dbl[..., R + N:])
            dt = jax.nn.softplus(jnp.einsum('blr,re->ble', dt_lo, W_dt) + b_dt)
            A = -jnp.exp(A_log)

            def step(h, inp):
                dt_t, B_t, C_t, u_t = inp
                dA = jnp.exp(dt_t[..., None] * A)
                h = dA * h + (dt_t * u_t)[..., None] * B_t[:, None, :]
                y_t = jnp.einsum('ben,bn->be', h, C_t)
                return (h, y_t)
            h0 = jnp.zeros((B, E, N), x.dtype)
            xs = (dt.transpose(1, 0, 2), Bm.transpose(1, 0, 2), Cm.transpose(1, 0, 2), u2.transpose(1, 0, 2))
            _, ys = lax.scan(step, h0, xs)
            y = ys.transpose(1, 0, 2) + u2 * D_param
            y = y * jax.nn.silu(z)
            out = jnp.einsum('ble,ed->bld', y, W_out)
            return x + res_scale * out
        return _mamba_block(x, ln_g, ln_b, W_in, conv_w, conv_b, W_xp, W_dt, b_dt, A_log, D_param, W_out, res_scale)

    def _L0_ffn_ref(x, k0, k1, k2, s0, s1, s2):
        import jax, jax.numpy as jnp
        import numpy as np
        import math
        D_IN = 128
        FEATURES = (512, 512, 128)
        BATCH, SEQ = (8, 256)

        def _conn_dense(kernel_bool, x):
            w = jnp.where(kernel_bool, jnp.float32(1.0), jnp.float32(-1.0))
            return x @ w
        h = jnp.concatenate([x, -x], axis=-1)
        h = s0 * _conn_dense(k0, h)
        h = jax.nn.relu(h) * 2
        h = s1 * _conn_dense(k1, h)
        h = jax.nn.relu(h) * 2
        h = s2 * _conn_dense(k2, h)
        return h
    x = L0_attn_a_x
    x = x + _L0_attn_a_ref(_layernorm(x, axis=-1), L0_attn_a_Wq, L0_attn_a_Wk, L0_attn_a_Wv, L0_attn_a_Wo)
    x = x + _L0_ffn_ref(_layernorm(x, axis=-1), L0_ffn_k0, L0_ffn_k1, L0_ffn_k2, L0_ffn_s0, L0_ffn_s1, L0_ffn_s2)
    x = x + _L0_attn_b_ref(_layernorm(x, axis=-1), L0_attn_b_ln_g, L0_attn_b_ln_b, L0_attn_b_W_in, L0_attn_b_conv_w, L0_attn_b_conv_b, L0_attn_b_W_xp, L0_attn_b_W_dt, L0_attn_b_b_dt, L0_attn_b_A_log, L0_attn_b_D_param, L0_attn_b_W_out, L0_attn_b_res_scale)
    x = x + _L0_ffn_ref(_layernorm(x, axis=-1), L0_ffn_k0, L0_ffn_k1, L0_ffn_k2, L0_ffn_s0, L0_ffn_s1, L0_ffn_s2)
    return x

_drawn_inputs = setup_inputs


def setup_inputs(seed=0):
    import zlib

    import numpy as np

    out = dict(_drawn_inputs(seed))
    spreads = {'L0_attn_b_ln_g': (1.0, 0.574),
     'L0_attn_b_ln_b': (0.0, 0.587),
     'L0_attn_b_conv_b': (0.0, 0.8),
     'L0_attn_b_D_param': (1.0, 0.6)}
    factors = {'L0_attn_b_W_dt': 3.376, 'L0_attn_b_b_dt': 3.887, 'L0_attn_b_A_log': 3.241}
    for name, (base, spread) in spreads.items():
        noise = np.random.default_rng([zlib.crc32(name.encode()), seed]).standard_normal(out[name].shape)
        drawn = base * np.exp(spread * noise) if base else spread * noise
        out[name] = jnp.asarray(drawn.astype(out[name].dtype))
    for name, factor in factors.items():
        out[name] = (out[name] * factor).astype(out[name].dtype)
    return out
```

```python
from contextlib import ExitStack

import numpy as np

import concourse.bass as bass
from concourse import mybir

F32 = mybir.dt.float32
BF16 = mybir.dt.bfloat16
F16 = mybir.dt.float16
U8 = mybir.dt.uint8
ALU = mybir.AluOpType
ACT = mybir.ActivationFunctionType
AX = mybir.AxisListType

NB, T, C, NH, HD = 4, 1024, 128, 16, 8
E2, NS, KC, RK = 2, 16, 4, 8
EPS = 1e-5
NEG = -1e30

CONST = {}
_at = 0
for _name, _n in (("ident", 128), ("e4", 128), ("e32", 32), ("hmask", 4), ("qmask", 4), ("idmod", 32), ("hsel", 128)):
    CONST[_name] = (_at, _n)
    _at += _n
NCONST = _at
NMASK = 3 * 512


def constants():
    out = np.zeros((128, NCONST + NMASK), np.float32)

    def put(name, a):
        at, n = CONST[name]
        out[: a.shape[0], at:at + n] = a.reshape(a.shape[0], n)

    p = np.arange(128)
    put("ident", np.eye(128, dtype=np.float32))
    q, k = np.arange(32)[:, None], np.arange(64)[None, :]
    win = np.where((k <= q + 32) & (k >= q + 1), 0.0, NEG)
    first = np.where((k <= q + 32) & (k >= q + 1) & (k >= 32), 0.0, NEG)
    r, c = np.arange(32)[:, None], np.arange(32)[None, :]
    stride = np.where((r // 16 == c // 16) & (c % 16 < r % 16), 0.0, NEG)
    head = np.concatenate([first] + [win] * 7, 1)
    rest = np.concatenate([win] * 8, 1)
    far = np.concatenate([stride] * 16, 1)
    out[:, NCONST:] = np.tile(np.concatenate([head, rest, far], 1), (4, 1))
    put("e4", (p[:, None] % 32 == p[None, :] % 32).astype(np.float32))
    put("e32", (p[:, None] % 32 == np.arange(32)[None, :]).astype(np.float32))
    put("hmask", (p[:, None] // 32 == np.arange(4)[None, :]).astype(np.float32))
    put("qmask", ((p[:, None] // 8 % 4 == np.arange(4)[None, :]) * float(HD) ** -0.5).astype(np.float32))
    put("idmod", (p[:96, None] % 32 == np.arange(32)[None, :]).astype(np.float32))
    put("hsel", (np.arange(16)[:, None] == p[None, :] // 8).astype(np.float32))
    return out


class Tok:

    def __init__(self, eng):
        self.eng, self.used, self.sem, self.value = eng, False, None, 0


class Queue:

    ENGINES = ("tensor", "vector", "scalar", "gpsimd", "sync")

    def __init__(self):
        self.ops = {e: [] for e in self.ENGINES}

    def add(self, eng, fn, waits, dma=False):
        tok = Tok(eng)
        tok.dma = dma
        flat = []
        stack = [waits]
        while stack:
            w = stack.pop()
            if w is None:
                continue
            if isinstance(w, Tok):
                w.used = True
                flat.append(w)
            else:
                stack.extend(w)
        self.ops[eng].append((flat, fn, tok))
        return tok

    def number(self, sem_of_engine, new_sem):
        for e, ops in self.ops.items():
            n = 0
            for _, _, tok in ops:
                if tok.dma:
                    tok.sem, tok.value = new_sem(), 16
                elif tok.used:
                    n += 1
                    tok.sem, tok.value = sem_of_engine[e], n

    def write(self, name, eng):
        seen = {}
        for waits, fn, tok in self.ops[name]:
            need = {}
            for w in waits:
                k = id(w.sem)
                if k not in need or need[k].value < w.value:
                    need[k] = w
            for k, w in need.items():
                if seen.get(k, 0) < w.value:
                    eng.wait_ge(w.sem, w.value)
                    seen[k] = w.value
            ins = fn(eng)
            if tok.dma:
                ins.then_inc(tok.sem, 16)
            elif tok.used:
                ins.then_inc(tok.sem, 1)


class Slots:

    def __init__(self, bufs):
        self.bufs, self.n, self.last, self.held = bufs, 0, [[] for _ in bufs], set()

    def take(self):
        i = self.n % len(self.bufs)
        self.n += 1
        assert i not in self.held
        self.held.add(i)
        w, self.last[i] = self.last[i], []
        return i, self.bufs[i], w

    def free(self, i, *toks):
        self.held.discard(i)
        self.last[i].extend(toks)


def hybrid_block(nc, ins, out):
    ctx = ExitStack()
    with ctx:
        def sb(name, shape, dt=F32):
            return ctx.enter_context(nc.sbuf_tensor(name, shape, dt))

        q = Queue()

        def pe(fn, *w):
            return q.add("tensor", fn, w)

        def dv(fn, *w):
            return q.add("vector", fn, w)

        def ac(fn, *w):
            return q.add("scalar", fn, w)

        def po(fn, *w):
            return q.add("gpsimd", fn, w)

        def dma(fn, *w):
            return q.add("sync", fn, w, dma=True)

        banks = [ctx.enter_context(nc.psum_tensor(f"ps{i}", [128, 512], F32)) for i in range(8)]
        PS = Slots(banks[0:4])
        Y = [banks[4], banks[5]]
        BB, CB = banks[6], banks[7]

        cst = sb("cst", [128, NCONST])

        def const(name, rows=128):
            at, n = CONST[name]
            return cst[0:rows, at:at + n]

        ident = const("ident")
        hmask = const("hmask")
        e32 = const("e32")
        masks = sb("masks", [128, 3, 512], BF16)
        e4 = sb("e4", [128, 128], BF16)
        idm = sb("idm", [96, 32], BF16)
        X = sb("X", [128, NB * 8, C])
        WT = sb("WT", [128, 4, 128])
        Win = sb("Win", [128, 512])
        Wk = sb("Wk", [128, KC, 256])
        Wxr = sb("Wxr", [128, 2, 40])
        Wx = sb("Wx", [128, 2, 104])
        Wdt = sb("Wdt", [128, 256])
        Wout = sb("Wout", [128, 2, 128])
        Al = sb("Al", [128, 2, NS])
        Ap = sb("Ap", [128, 2, NS])
        An = sb("An", [128, 2, NS])
        vec = sb("vec", [128, 16])
        bdt, cvb, Dp = vec[:, 0:2], vec[:, 2:4], vec[:, 4:6]
        lng, lnb, res = vec[:, 6:7], vec[:, 7:8], vec[:, 8:9]
        s3 = vec[:, 9:12]
        sgn = sb("sgn", [128, 8])
        fsc = sb("fsc", [128, 4])
        expo = sb("expo", [128, 8])
        w0 = sb("w0", [128, 512], F16)
        w1 = sb("w1", [128, 4, 512], F16)
        w2 = sb("w2", [128, 4, 128], F16)

        G = Slots([sb(f"g{i}", [128, 2, 512]) for i in range(4)])
        dA = Slots([sb(f"dA{i}", [128, 2, 512]) for i in range(2)])

        def flat(t):
            return t[:, :, :].rearrange("p a n -> p (a n)")

        mraw0, mraw1 = flat(G.bufs[0]), flat(G.bufs[1])
        cwr = flat(G.bufs[2])
        kraw = flat(G.bufs[3]).bitcast(U8)
        k0r = kraw[:, 0:1024].rearrange("p (a n) -> p a n", a=2)
        k1r = kraw[:, 1024:3072].rearrange("p (a n) -> p a n", a=4)
        k2r = kraw[:, 3072:3584].rearrange("p (a n) -> p a n", a=4)
        Wraw = flat(dA.bufs[0])[:, 0:512].rearrange("p (a n) -> p a n", a=4)
        kt = flat(dA.bufs[1])[:, 0:512]

        def load(dst, src):
            def go(e):
                with nc.allow_non_contiguous_dma(reason="small vectors"):
                    return e.dma_start(dst, src)
            return dma(go)

        l_x = [None] * NB

        def load_x(b):
            l_x[b] = load(X[:, 8 * b:8 * b + 8, :], ins["x"][b].rearrange("(i p) c -> p i c", p=128))

        load_x(0)
        l_cst = load(cst[:, :], ins["consts"][:, 0:NCONST])
        l_m = [load(mraw0, ins["consts"][:, NCONST:NCONST + 1024]), load(mraw1[:, 0:512], ins["consts"][:, NCONST + 1024:])]
        l_w = [load(Wraw[:, i, :], ins[n]) for i, n in enumerate(("Wq", "Wk", "Wv", "Wo"))]
        l_s = [load(vec[:, 9 + i:10 + i], ins[f"s{i}"].to_broadcast((128, 1))) for i in range(3)]
        l_k0 = load(k0r, ins["k0"].rearrange("(a p) n -> p a n", p=128))
        l_k1 = load(k1r, ins["k1"].rearrange("(a p) n -> p a n", p=128))
        l_k2 = load(k2r, ins["k2"].rearrange("(a p) n -> p a n", p=128))
        l_win = load(Win[:, :], ins["W_in"])
        l_cw = load(cwr, ins["conv_w"].rearrange("(o e) k -> o (e k)", o=1).to_broadcast((128, 256 * KC)))
        l_wx = load(Wxr[:, :, :], ins["W_xp"].rearrange("(a p) n -> p a n", p=128))
        l_wdt = load(Wdt[96:104, :], ins["W_dt"])
        l_wo = load(Wout[:, :, :], ins["W_out"].rearrange("(a p) n -> p a n", p=128))
        l_al = load(Al[:, :, :], ins["A_log"].rearrange("(a p) n -> p a n", p=128))
        l_v = [load(vec[:, 2 * i:2 * i + 2], ins[n].rearrange("(a p) -> p a", p=128))
               for i, n in enumerate(("b_dt", "conv_b", "D_param"))]
        l_v += [load(vec[:, 6 + i:7 + i], ins[n].rearrange("(p o) -> p o", o=1)) for i, n in enumerate(("ln_g", "ln_b"))]
        l_res = load(vec[:, 8:9], ins["res"].to_broadcast((128, 1)))
        for b in range(1, NB):
            load_x(b)

        mk_ = masks[:, :, :].rearrange("p a n -> p (a n)")
        c_mask = [dv(lambda e: e.tensor_copy(mk_[:, 0:1024], mraw0), l_m[0]), dv(lambda e: e.tensor_copy(mk_[:, 1024:1536], mraw1[:, 0:512]), l_m[1])]
        c_e4 = po(lambda e: e.tensor_scalar(e4[:, :], const("e4"), 1.0, None, ALU.mult), l_cst)
        c_sel = dv(lambda e: e.tensor_copy(idm[:, :], const("idmod", 96)), l_cst)
        c_expo = po(lambda e: e.memset(expo[:, :], -0.5))
        i, bank, w = PS.take()
        for j in range(4):
            t_w = pe(lambda e, j=j, bank=bank: e.transpose(bank[:, 128 * j:128 * j + 128], Wraw[:, j, :], ident), l_w[j], l_cst, w)
        c_wt = ac(lambda e, bank=bank: e.copy(WT[:, :, :].rearrange("p a n -> p (a n)"), bank[:, :]), t_w)
        PS.free(i, c_wt)
        dA.free(0, t_w)

        g1 = dv(lambda e: e.tensor_scalar(sgn[:, 0:3], s3, 0.0, None, ALU.is_gt), l_s)
        g2 = dv(lambda e: e.tensor_scalar(sgn[:, 3:6], s3, 0.0, None, ALU.is_lt), l_s)
        g3 = dv(lambda e: e.tensor_tensor(sgn[:, 0:3], sgn[:, 0:3], sgn[:, 3:6], ALU.subtract), g1, g2)
        g4 = dv(lambda e: e.tensor_tensor(fsc[:, 0:3], sgn[:, 0:3], s3, ALU.mult), g3)
        g5 = dv(lambda e: e.tensor_tensor(fsc[:, 3:4], fsc[:, 0:1], fsc[:, 1:2], ALU.mult), g4)
        c_f = dv(lambda e: e.tensor_scalar(fsc[:, 3:4], fsc[:, 3:4], s3[:, 2:3], 64.0, ALU.mult, ALU.mult), g5)
        FS = fsc[:, 3:4]
        g6 = dv(lambda e: e.tensor_scalar(sgn[:, 3:5], sgn[:, 0:2], 2.0, None, ALU.mult), g3)
        g7 = dv(lambda e: e.tensor_scalar(sgn[:, 4:5], sgn[:, 1:2], 0.125, None, ALU.mult), g6)
        g8 = dv(lambda e: e.tensor_tensor(kt, k0r[:, 0, :], k0r[:, 1, :], ALU.subtract), l_k0)
        c_w0 = dv(lambda e: e.tensor_scalar(w0[:, :], kt, sgn[:, 3:4], None, ALU.mult), g8, g6)
        c_w1 = dv(lambda e: e.tensor_scalar(w1[:, :, :].rearrange("p a n -> p (a n)"), kraw[:, 1024:3072],
                                            0.5, sgn[:, 4:5], ALU.subtract, ALU.mult), g7, l_k1)
        c_w2 = dv(lambda e: e.tensor_scalar(w2[:, :, :].rearrange("p a n -> p (a n)"), kraw[:, 3072:3584],
                                            2.0, 1.0, ALU.mult, ALU.subtract), l_k2)

        cwv = cwr.rearrange("p (e k) -> p k e", k=KC)
        c_wk = dv(lambda e: e.tensor_tensor(Wk[:, :, :], cwv, Win[:, 0:256].unsqueeze(1).to_broadcast((128, KC, 256)), ALU.mult),
                  l_win, l_cw)
        G.free(0, c_mask)
        G.free(1, c_mask)
        G.free(2, c_wk)
        G.free(3, c_w0, c_w1, c_w2)
        dA.free(1, c_w0)
        wx = [dv(lambda e, r=r: e.tensor_copy(Wx[:, :, 32 * r:32 * r + 32], Wxr[:, :, 8:40]), l_wx) for r in range(3)]
        wx.append(dv(lambda e: e.tensor_copy(Wx[:, :, 96:104], Wxr[:, :, 0:8]), l_wx))
        a1 = ac(lambda e: e.activation(Ap[:, :, :], Al[:, :, :], ACT.Exp), l_al)
        c_an = dv(lambda e: e.tensor_scalar(An[:, :, :], Ap[:, :, :], -1.0, None, ALU.mult), a1)

        xready = [[l_x[b]] for b in range(NB)]

        st = Slots([sb(f"st{i}", [128, 8, 6]) for i in range(2)])
        mv = Slots([sb(f"mv{i}", [128, 8, 2]) for i in range(2)])
        rs = Slots([sb(f"rs{i}", [128, 2, 8]) for i in range(2)])
        LNO = Slots([sb("lno", [128, 8, C])])
        LNM = Slots([sb("lnm", [128, 8, C])])

        aT = sb("aT", [128, 32 + T])
        KT = sb("KT", [128, 32 + T])
        aP = sb("aP", [128, T])
        QT = sb("QT", [128, T])
        QM = Slots([sb(f"qm{i}", [128, 8, 4, 32]) for i in range(2)])
        V1 = Slots([sb(f"v1{i}", [128, 4, 2, 4, 33]) for i in range(2)])
        V2 = Slots([sb("v2", [128, 4, 4, 4, 33])])
        Sx = Slots([sb(f"sx{i}", [128, 512]) for i in range(2)])
        PT = Slots([sb(f"pt{i}", [128, 4, 128]) for i in range(2)])
        mx = Slots([sb(f"mx{i}", [128, 16]) for i in range(4)])
        OM = Slots([sb(f"om{i}", [128, 16, 4, 32]) for i in range(1)])
        LM = Slots([sb(f"lm{i}", [128, 2, 16, 4, 4]) for i in range(1)])
        far = sb("far", [128, T])
        farc = sb("farc", [16, 2, T])
        near = Slots([sb(f"near{i}", [128, 256]) for i in range(1)])
        nearc = Slots([sb(f"nearc{i}", [16, 2, 256]) for i in range(1)])
        tmp = sb("tmp", [128, 2, 256])
        tmc = sb("tmc", [16, 4, 256])

        FA = Slots([sb(f"fa{i}", [128, 2, 512], F16) for i in range(1)])
        H0 = Slots([sb(f"h0{i}", [128, 2, 4, 512], F16) for i in range(1)])
        H1 = Slots([sb(f"h1{i}", [128, 2, 4, 512], F16) for i in range(1)])

        xnT = sb("xnT", [128, 4 + T])
        zs = sb("zs", [128, 2, T])
        u2 = sb("u2", [128, 2, T])
        dtb = sb("dtb", [128, 2, T])
        dtu = sb("dtu", [128, 2, T])
        BC = sb("BC", [96, T], BF16)
        hl = sb("hl", [128, 2, NS])

        z = [po(lambda e: e.memset(aT[:, 0:32], 0.0)), po(lambda e: e.memset(KT[:, 0:32], 0.0)),
             po(lambda e: e.memset(xnT[:, 0:4], 0.0)), po(lambda e: e.memset(hl[:, :, :], 0.0))]
        ones = []
        for v, n in ((V1.bufs[0], 2), (V1.bufs[1], 2), (V2.bufs[0], 4)):
            zv = po(lambda e, v=v: e.memset(v[:, :, :, :, :], 0.0))
            r = 128 // n
            ones += [dv(lambda e, k=k, v=v, r=r: e.memset(v[r * k:r * k + r, :, k, :, 32], 1.0), zv) for k in range(n)]
        c_z = z + ones

        def norm(src, ready, dst, dwait):
            i1, s_, w1_ = st.take()
            i2, m_, w2_ = mv.take()
            i3, r_, w3_ = rs.take()
            ag = []
            ss = [dv(lambda e, k=k: e.bn_stats(s_[:, k, :], src(k)), ready, w1_) for k in range(8)]
            for k in range(8):
                ag.append(dv(lambda e, k=k: e.bn_aggr(m_[:, k, :], s_[:, k, :]), ss[k], w2_))
            st.free(i1, *ag)
            a = po(lambda e: e.tensor_scalar(r_[:, 1, :], m_[:, :, 1], 1.0, EPS, ALU.mult, ALU.add), ag, w3_)
            p = po(lambda e: e.tensor_tensor(r_[:, 0, :], r_[:, 1, :], expo[:, :], ALU.pow), a, c_expo)
            m1 = po(lambda e: e.tensor_tensor(r_[:, 1, :], m_[:, :, 0], r_[:, 0, :], ALU.mult), p)
            m2 = po(lambda e: e.tensor_scalar(r_[:, 1, :], r_[:, 1, :], -1.0, 0.0, ALU.mult, ALU.add), m1)
            mv.free(i2, m1)
            o = [po(lambda e, k=k: e.tensor_scalar(dst[:, k, :], src(k), r_[:, 0, k:k + 1], r_[:, 1, k:k + 1], ALU.mult, ALU.add),
                    m2, ready, dwait) for k in range(8)]
            rs.free(i3, *o)
            return o

        state = {"attn_in": [], "attn_v": [], "olm": [], "qk": [], "tmp": [], "xnT": [], "XA": [], "zs": [], "u2": [],
                 "dt": [], "BC": [], "y": [], "bb": [], "cb": [], "hl": [], "yg": [], "dlo": [], "Hs": [], "Ms": [], "Rs": [], "sp": [[], [], [], []]}

        def attention(b):
            S = state
            il, A, wl = LNO.take()
            no = norm(lambda k: X[:, 8 * b + k, :], xready[b], A, wl)
            yield
            tr, cp = [], []
            for h in range(2):
                i, bank, w = PS.take()
                for k in range(4):
                    t = pe(lambda e, k=k, h=h, bank=bank: e.transpose(bank[:, 128 * k:128 * k + 128], A[:, 4 * h + k, :], ident),
                           no[4 * h + k], w, l_cst)
                    tr.append(t)
                c = ac(lambda e, h=h, bank=bank: e.copy(aT[:, 32 + 512 * h:32 + 512 * h + 512], bank[:, :]), t, S["attn_in"], c_z)
                cp.append(c)
                PS.free(i, c)
            aPd = [po(lambda e, g=g: e.tensor_scalar(
                aP[:, 512 * g:512 * g + 512].rearrange("p (r j) -> p r j", j=16),
                aT[:, 32:32 + T].rearrange("p (j r) -> p r j", r=64)[:, 32 * g:32 * g + 32, :], 1.0, 0.0, ALU.mult, ALU.add),
                cp, S["attn_in"]) for g in range(2)]
            LNO.free(il, *tr)
            yield
            qk_done, q_done, k_done = [], [], []
            for h in range(2):
                i, bank, w = PS.take()
                t = pe(lambda e, h=h, bank=bank: e.matmul(bank[:, :], WT[:, 0, :], aT[:, 32 + 512 * h:544 + 512 * h], start=True, stop=True),
                       c_wt, cp, w)
                qk_done.append(t)
                c = ac(lambda e, h=h, bank=bank: e.copy(QT[:, 512 * h:512 * h + 512], bank[:, :]), t, S["qk"])
                q_done.append(c)
                PS.free(i, c)
                i, bank, w = PS.take()
                t = pe(lambda e, h=h, bank=bank: e.matmul(bank[:, :], WT[:, 1, :], aT[:, 32 + 512 * h:544 + 512 * h], start=True, stop=True), w)
                qk_done.append(t)
                c = ac(lambda e, h=h, bank=bank: e.copy(KT[:, 32 + 512 * h:544 + 512 * h], bank[:, :]), t, S["qk"], c_z)
                k_done.append(c)
                PS.free(i, c)
                yield
            aw = aT[:, :]

            def values(kind, g, cp=cp):
                i, bank, w = PS.take()
                iv, V, wv = (V1, V2)[kind].take()
                for k in range(4):
                    m = 4 * g + k
                    if kind:
                        t = pe(lambda e, k=k, m=m, bank=bank: e.matmul(
                            bank[:, 128 * k:128 * k + 128], aP[:, 128 * m:128 * m + 128], WT[:, 2, :], start=True, stop=True), aPd, w)
                        continue
                    for s in range(2):
                        t = pe(lambda e, k=k, m=m, s=s, bank=bank: e.matmul(
                            bank[64 * s:64 * s + 64, 128 * k:128 * k + 128],
                            aw[:, 64 * m + 32 * s:64 * m + 32 * s + 64], WT[:, 2, :], start=True, stop=True), cp, w)
                qk_done.append(t)
                r = (64, 32)[kind]
                vs = [ac(lambda e, s=s: e.copy(V[r * s:r * s + r, :, s, :, 0:32],
                                               bank[r * s:r * s + r, :].rearrange("p (k a d) -> p k a d", k=4, a=4)), t, wv, c_z)
                      for s in range(128 // r)]
                PS.free(i, *vs)
                return iv, V, vs

            Qs = QT[:, :].rearrange("p (j r) -> p r j", r=64)
            qmask = const("qmask")
            Ks = KT[:, 32:32 + T].rearrange("p (j r) -> p r j", r=64)
            s_last, farm, merged, atts, q_read = [], [], [], [], []
            for kind in (1, 0):
                nq, kw, nw = ((8, 64, 2), (16, 32, 4))[kind]
                for g in range((4, 2)[kind]):
                    io, om, wo_ = OM.take()
                    im, lm, wm_ = LM.take()
                    iv, V, v_done = values(kind, g)
                    qm, qm_done = [], []
                    for s in range(nq // 8):
                        iq, qt, wq = QM.take()
                        at = nq * g + 8 * s
                        qm.append((iq, qt))
                        for j in range(4):
                            if kind:
                                src = Qs[:, 2 * at:2 * at + 16, :].rearrange("p (a r) j -> p a r j", r=2)
                                dst = qt[:, :, j, :].rearrange("p a (r j) -> p a r j", r=2)
                            else:
                                src = QT[:, 32 * at:32 * at + 256].rearrange("p (a n) -> p a n", n=32)
                                dst = qt[:, :, j, :]
                            qm_done.append(po(lambda e, src=src, dst=dst, j=j: e.tensor_scalar(dst, src, qmask[:, j:j + 1], 0.0, ALU.mult, ALU.add),
                                              q_done, wq, l_cst))
                    q_read += qm_done
                    packed = []
                    for hg in range(4):
                        r0 = 32 * hg
                        i, bank, w = PS.take()
                        mk = 2 if kind else (0 if g == 0 else 1)
                        pe(lambda e, r0=r0, mk=mk, bank=bank: e.matmul(bank[:, :], e4[r0:r0 + 32, :], masks[r0:r0 + 32, mk, :], start=True,
                                                                      stop=False, skip_group_check=True), c_mask, c_e4, w)
                        for k in range(nq):
                            m = nq * g + k
                            lq = qm[k // 8][1][r0:r0 + 32, k % 8, :, :].rearrange("p a n -> p (a n)")
                            if kind == 0:
                                rk = KT[r0:r0 + 32, 32 * m:32 * m + 64]
                            else:
                                rk = Ks[r0:r0 + 32, 2 * m:2 * m + 2, :]
                            t = pe(lambda e, lq=lq, rk=rk, k=k, kw=kw, nq=nq, bank=bank: e.matmul(
                                bank[:, kw * k:kw * k + kw], lq, rk, start=False, stop=(k == nq - 1), skip_group_check=True), qm_done, k_done)
                        s_last.append(t)
                        ix, mm, wx_ = mx.take()
                        sv = bank[:, :].rearrange("p (a k) -> p a k", k=kw)
                        t = dv(lambda e, mm=mm, sv=sv, nq=nq: e.tensor_reduce(mm[:, 0:nq], sv, AX.X, ALU.max), t, wx_)
                        isx, sx, ws_ = Sx.take()
                        t2 = dv(lambda e, mm=mm, sv=sv, sx=sx, nq=nq, kw=kw: e.tensor_tensor(
                            sx[:, :].rearrange("p (a k) -> p a k", k=kw), sv, mm[:, 0:nq].unsqueeze(2).to_broadcast((128, nq, kw)),
                            ALU.subtract), t, ws_)
                        PS.free(i, t2)
                        pk = dv(lambda e, mm=mm, lm=lm, hg=hg, nq=nq: e.tensor_tensor(
                            lm[:, 1, 0:nq, hg, :], mm[:, 0:nq].unsqueeze(2).to_broadcast((128, nq, 4)),
                            hmask.unsqueeze(1).to_broadcast((128, nq, 4)), ALU.mult), t, wm_)
                        mx.free(ix, pk, t2)
                        packed.append(pk)
                        t3 = ac(lambda e, sx=sx: e.activation(sx[:, :], sx[:, :], ACT.Exp), t2)
                        i, bank, w = PS.take()
                        for k in range(4):
                            t4 = pe(lambda e, k=k, bank=bank, sx=sx: e.transpose(bank[:, 128 * k:128 * k + 128], sx[:, 128 * k:128 * k + 128], ident),
                                    t3, w)
                        Sx.free(isx, t4)
                        ip, pt, wp_ = PT.take()
                        t5 = ac(lambda e, pt=pt, bank=bank: e.copy(pt[:, :, :].rearrange("p a n -> p (a n)"), bank[:, :]), t4, wp_)
                        PS.free(i, t5)
                        per = (4, 2)[kind]
                        for o in range(4 // per):
                            i, bank, w = PS.take()
                            for k in range(per):
                                kk = per * o + k
                                t6 = pe(lambda e, k=k, kk=kk, bank=bank, pt=pt, g=g, hg=hg, nw=nw, V=V: e.matmul(
                                    bank[:, 33 * nw * k:33 * nw * (k + 1)], pt[:, kk, :], V[:, kk, :, hg, :], start=True, stop=True),
                                    t5, v_done, w)
                            ov = bank[:, 0:33 * nw * per].rearrange("p (a n) -> p a n", n=33)
                            a0, na = nw * per * o, nw * per
                            t7 = dv(lambda e, ov=ov, om=om, a0=a0, na=na, hg=hg: e.tensor_tensor(
                                om[:, a0:a0 + na, hg, :].rearrange("p a (h d) -> p a h d", h=4), ov[:, :, 0:32].rearrange("p a (h d) -> p a h d", h=4),
                                hmask.unsqueeze(1).unsqueeze(3).to_broadcast((128, na, 4, 8)), ALU.mult), t6, wo_)
                            t8 = dv(lambda e, ov=ov, lm=lm, a0=a0, na=na, hg=hg: e.tensor_tensor(
                                lm[:, 0, a0:a0 + na, hg, :], ov[:, :, 32:33].to_broadcast((128, na, 4)),
                                hmask.unsqueeze(1).to_broadcast((128, na, 4)), ALU.mult), t6, wm_)
                            PS.free(i, t7, t8)
                            packed += [t7, t8]
                        PT.free(ip, t6)
                        yield
                    (V1, V2)[kind].free(iv, t6)
                    for iq, _ in qm:
                        QM.free(iq, s_last[-1])
                    done = []
                    for s in range(nq // 8):
                        i1, b1, wa = PS.take()
                        i2, b2, wb = PS.take()
                        for k in range(8):
                            a = 8 * s + k
                            t1 = pe(lambda e, k=k, a=a, b1=b1, om=om: e.matmul(
                                b1[:, 32 * k:32 * k + 32], om[:, a, :, :].rearrange("p a n -> p (a n)"), e32, start=True, stop=True), packed, wa)
                        for x in range(2):
                            for k in range(8):
                                a = 8 * s + k
                                t2 = pe(lambda e, k=k, a=a, x=x, b2=b2, lm=lm: e.matmul(
                                    b2[0:16, 256 * x + 32 * k:256 * x + 32 * k + 32], lm[:, x, a, :, :].rearrange("p a b -> p (a b)"),
                                    e32, start=True, stop=True), wb)
                        at = nq * g + 8 * s
                        if kind == 0:
                            olm = []
                            inr, nr, wn = near.take()
                            inc, nc_, wnc = nearc.take()
                            c1 = ac(lambda e, nr=nr, b1=b1: e.copy(nr[:, :], b1[:, 0:256]), t1, wn)
                            c2 = ac(lambda e, nc_=nc_, b2=b2: e.copy(nc_[:, :, :].rearrange("p a n -> p (a n)"), b2[0:16, :]), t2, wnc)
                            olm += [c1, c2]
                        else:
                            dst = far[:, :].rearrange("p (j r) -> p r j", r=64)[:, 2 * at:2 * at + 16, :]
                            v1 = b1[:, 0:256].rearrange("p (r j) -> p r j", j=16)
                            c1 = ac(lambda e, dst=dst, v1=v1: e.copy(dst, v1), t1, S["olm"])
                            dsc = farc[:, :, :].rearrange("p a (j r) -> p a r j", r=64)[:, :, 2 * at:2 * at + 16, :]
                            v2 = b2[0:16, :].rearrange("p (a r j) -> p a r j", a=2, j=16)
                            for x in range(2):
                                c2 = ac(lambda e, x=x, dsc=dsc, v2=v2: e.copy(dsc[:, x, :, :], v2[:, x, :, :]), t2, S["olm"])
                                farm.append(c2)
                            farm.append(c1)
                        PS.free(i1, c1)
                        PS.free(i2, c2)
                        done += [t1, t2]
                    OM.free(io, *done)
                    LM.free(im, *done)
                    yield
                    if kind:
                        continue
                    cols = slice(256 * g, 256 * g + 256)
                    L1, M1 = nc_[:, 0, :], nc_[:, 1, :]
                    L2, M2 = farc[:, 0, cols], farc[:, 1, cols]
                    ta = dv(lambda e, M1=M1, M2=M2: e.tensor_tensor(tmc[:, 2, :], M1, M2, ALU.max), olm, farm, S["tmp"])
                    tb = po(lambda e, M1=M1: e.tensor_tensor(tmc[:, 0, :], M1, tmc[:, 2, :], ALU.subtract), ta)
                    tc_ = po(lambda e, M2=M2: e.tensor_tensor(tmc[:, 1, :], M2, tmc[:, 2, :], ALU.subtract), ta)
                    td = ac(lambda e: e.activation(tmc[:, 0:2, :], tmc[:, 0:2, :], ACT.Exp), tb, tc_)
                    f1 = po(lambda e, L1=L1: e.tensor_tensor(tmc[:, 2, :], L1, tmc[:, 0, :], ALU.mult), td)
                    f2 = po(lambda e, L2=L2: e.tensor_tensor(tmc[:, 3, :], L2, tmc[:, 1, :], ALU.mult), td)
                    f3 = po(lambda e: e.tensor_tensor(tmc[:, 2, :], tmc[:, 2, :], tmc[:, 3, :], ALU.add), f1, f2)
                    yield
                    f4 = dv(lambda e: e.reciprocal(tmc[:, 2, :], tmc[:, 2, :]), f3)
                    f5 = po(lambda e: e.tensor_tensor(tmc[:, 0, :], tmc[:, 0, :], tmc[:, 2, :], ALU.mult), f4)
                    f6 = po(lambda e: e.tensor_tensor(tmc[:, 1, :], tmc[:, 1, :], tmc[:, 2, :], ALU.mult), f4)
                    nearc.free(inc, f1, ta, tb)
                    i, bank, w = PS.take()
                    f7 = pe(lambda e, bank=bank: e.matmul(bank[:, :], const("hsel", 16), tmc[:, 0:2, :], start=True, stop=True), f5, f6, w)
                    yield
                    O2 = far[:, cols]
                    ATT = tmp[:, 0, :]
                    h1 = dv(lambda e, bank=bank, nr=nr: e.tensor_tensor(tmp[:, 0, :], bank[:, 0:256], nr[:, :], ALU.mult), f7)
                    h2 = dv(lambda e, bank=bank, O2=O2: e.tensor_tensor(tmp[:, 1, :], bank[:, 256:512], O2, ALU.mult), f7)
                    PS.free(i, h1, h2)
                    f8 = dv(lambda e: e.tensor_tensor(tmp[:, 0, :], tmp[:, 0, :], tmp[:, 1, :], ALU.add), h1, h2)
                    near.free(inr, h1)
                    merged += [h2, f2, ta, tc_]
                    i, bank, w = PS.take()
                    for k in range(2):
                        t = pe(lambda e, k=k, bank=bank: e.matmul(bank[:, 128 * k:128 * k + 128], ATT[:, 128 * k:128 * k + 128], WT[:, 3, :],
                                                                 start=True, stop=True), f8, w)
                    xv = X[:, 8 * b + 2 * g:8 * b + 2 * g + 2, :].rearrange("p a c -> p (a c)")
                    x1 = dv(lambda e, xv=xv, bank=bank: e.tensor_tensor(xv, bank[:, 0:256], xv, ALU.add), t, no)
                    PS.free(i, x1)
                    atts.append(x1)
                    S["tmp"] = [t, f7]
                    yield
            S["attn_in"] = qk_done + aPd
            S["qk"] = s_last + q_read
            S["olm"] = merged
            xready[b] = atts

        def ffn(b):
            il, A, wl = LNO.take()
            no = norm(lambda k: X[:, 8 * b + k, :], xready[b], A, wl)
            yield
            xs, trs = [], []
            for h in range(2):
                i, bank, w = PS.take()
                for k in range(4):
                    t = pe(lambda e, k=k, h=h, bank=bank: e.transpose(bank[:, 128 * k:128 * k + 128], A[:, 4 * h + k, :], ident),
                           no[4 * h + k], w, l_cst)
                trs.append(t)
                ia, fa, wa = FA.take()
                c1 = ac(lambda e, fa=fa, bank=bank: e.copy(fa[:, 0, :], bank[:, :]), t, wa)
                c2 = dv(lambda e, fa=fa, bank=bank: e.tensor_tensor(fa[:, 1, :], bank[:, :], fa[:, 0, :], ALU.subtract), c1, wa)
                PS.free(i, c2)
                ih, h0, wh = H0.take()
                r0 = []
                for mo in range(4):
                    i, bank, w = PS.take()
                    for s in range(2):
                        t = pe(lambda e, s=s, mo=mo, fa=fa, bank=bank: e.matmul(bank[:, :], w0[:, 128 * mo:128 * mo + 128], fa[:, s, :],
                                                                               start=(s == 0), stop=(s == 1)), c1, c2, c_w0, w)
                    e1 = ac(lambda e, mo=mo, h0=h0, bank=bank: e.activation(h0[:, 0, mo, :], bank[:, :], ACT.Relu), t, wh)
                    e2 = dv(lambda e, mo=mo, h0=h0, bank=bank: e.scalar_tensor_tensor(h0[:, 1, mo, :], bank[:, :], 0.0, h0[:, 0, mo, :],
                                                                                    ALU.max, ALU.subtract), e1, wh)
                    PS.free(i, e2)
                    r0.append(e2)
                    yield
                FA.free(ia, t)
                i1, h1, wh1 = H1.take()
                r1 = []
                for mo in range(4):
                    i, bank, w = PS.take()
                    n = 0
                    for ki in range(4):
                        for s in range(2):
                            t = pe(lambda e, s=s, mo=mo, ki=ki, n=n, h0=h0, bank=bank: e.matmul(
                                bank[:, :], w1[:, ki, 128 * mo:128 * mo + 128], h0[:, s, ki, :], start=(n == 0), stop=(n == 7)), r0[ki], c_w1, w)
                            n += 1
                    e1 = ac(lambda e, mo=mo, h1=h1, bank=bank: e.activation(h1[:, 0, mo, :], bank[:, :], ACT.Relu), t, wh1)
                    e2 = dv(lambda e, mo=mo, h1=h1, bank=bank: e.scalar_tensor_tensor(h1[:, 1, mo, :], bank[:, :], 0.0, h1[:, 0, mo, :],
                                                                                    ALU.max, ALU.subtract), e1, wh1)
                    PS.free(i, e2)
                    r1.append(e2)
                    yield
                H0.free(ih, t)
                i, bank, w = PS.take()
                for k in range(4):
                    n = 0
                    for ki in range(4):
                        for s in range(2):
                            t = pe(lambda e, s=s, k=k, ki=ki, n=n, h1=h1, bank=bank: e.matmul(
                                bank[:, 128 * k:128 * k + 128], h1[:, s, ki, 128 * k:128 * k + 128], w2[:, ki, :],
                                start=(n == 0), stop=(n == 7)), r1[ki], c_w2, w)
                            n += 1
                H1.free(i1, t)
                xv = X[:, 8 * b + 4 * h:8 * b + 4 * h + 4, :].rearrange("p a c -> p (a c)")
                x1 = dv(lambda e, xv=xv, bank=bank: e.scalar_tensor_tensor(xv, bank[:, :], FS, xv, ALU.mult, ALU.add), t, no, c_f)
                PS.free(i, x1)
                xs.append(x1)
                yield
            LNO.free(il, *trs)
            xready[b] = xs

        def mamba(b):
            S = state
            il, A, wl = LNM.take()
            no = norm(lambda k: X[:, 8 * b + k, :], xready[b], A, wl)
            yield
            Xf = X[:, 8 * b:8 * b + 8, :].rearrange("p a c -> p (a c)")
            xa = po(lambda e: e.tensor_tensor(Xf, Xf, A[:, :, :].rearrange("p a c -> p (a c)"), ALU.add), no)
            no2 = norm(lambda k: A[:, k, :], no, A, xa)
            yield
            trs, cp = [], []
            for h in range(2):
                i, bank, w = PS.take()
                for k in range(4):
                    t = pe(lambda e, k=k, h=h, bank=bank: e.transpose(bank[:, 128 * k:128 * k + 128], A[:, 4 * h + k, :], ident),
                           no2[4 * h + k], w)
                trs.append(t)
                c = ac(lambda e, h=h, bank=bank: e.activation(xnT[:, 4 + 512 * h:516 + 512 * h], bank[:, :], ACT.Identity, bias=lnb, scale=lng),
                       t, S["xnT"], l_v, c_z)
                PS.free(i, c)
                cp.append(c)
            LNM.free(il, *trs)
            yield
            zz, uu, pr = [], [], []
            for h in range(2):
                for eb in range(2):
                    i, bank, w = PS.take()
                    t = pe(lambda e, h=h, eb=eb, bank=bank: e.matmul(bank[:, :], Win[:, 256 + 128 * eb:384 + 128 * eb],
                                                                    xnT[:, 4 + 512 * h:516 + 512 * h], start=True, stop=True), cp, l_win, w)
                    c = ac(lambda e, h=h, eb=eb, bank=bank: e.activation(zs[:, eb, 512 * h:512 * h + 512], bank[:, :], ACT.Silu), t, S["zs"])
                    PS.free(i, c)
                    zz.append(c)
                    i, bank, w = PS.take()
                    for k in range(KC):
                        t = pe(lambda e, k=k, h=h, eb=eb, bank=bank: e.matmul(
                            bank[:, :], Wk[:, k, 128 * eb:128 * eb + 128], xnT[:, 1 + k + 512 * h:513 + k + 512 * h],
                            start=(k == 0), stop=(k == KC - 1)), c_wk, w)
                    c = ac(lambda e, h=h, eb=eb, bank=bank: e.activation(u2[:, eb, 512 * h:512 * h + 512], bank[:, :], ACT.Silu,
                                                                        bias=cvb[:, eb:eb + 1]), t, S["u2"])
                    PS.free(i, c)
                    uu.append(c)
                    pr.append(t)
                    yield
            S["xnT"] = pr
            bc, dtd, dud = [], [], []
            for h in range(2):
                hs = slice(512 * h, 512 * h + 512)
                i, bank, w = PS.take()
                for eb in range(2):
                    t = pe(lambda e, eb=eb, hs=hs, bank=bank: e.matmul(bank[0:104, :], Wx[:, eb, :], u2[:, eb, hs],
                                                                      start=(eb == 0), stop=(eb == 1)), uu, wx, w)
                jr, rb, wr = G.take()
                Rs = rb[:, 0, :]
                hm_ = rb[:, 1, :].bitcast(BF16)
                Hs, Ms = hm_[0:96, 0:512], hm_[0:96, 512:1024]
                c0 = ac(lambda e, bank=bank, Rs=Rs: e.copy(Rs[96:104, :], bank[96:104, :]), t, wr)
                c1 = ac(lambda e, bank=bank, Hs=Hs: e.copy(Hs, bank[0:96, :]), t, wr)
                c2 = dv(lambda e, bank=bank, Rs=Rs, Hs=Hs: e.tensor_tensor(Rs[0:96, :], bank[0:96, :], Hs, ALU.subtract), c1)
                PS.free(i, c0, c2)
                c3 = dv(lambda e, Rs=Rs, Ms=Ms: e.tensor_copy(Ms, Rs[0:96, :]), c2)
                c4 = dv(lambda e, hs=hs, Rs=Rs, Ms=Ms: e.tensor_tensor(BC[64:96, hs], Rs[64:96, :], Ms[64:96, :], ALU.subtract), c3, S["BC"])
                c5 = ac(lambda e, hs=hs, Hs=Hs: e.copy(BC[0:32, hs], Hs[0:32, :]), c1, S["BC"])
                c6 = ac(lambda e, hs=hs, Ms=Ms: e.copy(BC[32:64, hs], Ms[32:64, :]), c3, S["BC"])
                bc += [c4, c5, c6]
                for eb in range(2):
                    i, bank, w = PS.take()
                    t = pe(lambda e, eb=eb, bank=bank, Rs=Rs: e.matmul(bank[:, :], Wdt[96:104, 128 * eb:128 * eb + 128], Rs[96:104, :],
                                                               start=True, stop=True), c0, l_wdt, w)
                    bb = bdt[:, eb:eb + 1]
                    ja, pa, wpa = dA.take()
                    jb, pb, wpb = G.take()
                    s0_, s1_, s2_, s3_ = pa[:, 0:1, :], pa[:, 1:2, :], pb[:, 0:1, :], pb[:, 1:2, :]
                    s0_, s1_, s2_, s3_ = (v.rearrange("p a n -> p (a n)") for v in (s0_, s1_, s2_, s3_))
                    d1 = ac(lambda e, s0_=s0_, s1_=s1_, s2_=s2_, s3_=s3_, bank=bank, bb=bb: e.activation(s0_, bank[:, :], ACT.Relu, bias=bb), t, wpa)
                    d2 = ac(lambda e, s0_=s0_, s1_=s1_, s2_=s2_, s3_=s3_, bank=bank, bb=bb: e.activation(s1_, bank[:, :], ACT.Abs, bias=bb), t, wpa)
                    PS.free(i, d1, d2)
                    d3 = ac(lambda e, s0_=s0_, s1_=s1_, s2_=s2_, s3_=s3_: e.activation(s1_, s1_, ACT.Exp, scale=-1.0), d2)
                    d4 = dv(lambda e, s0_=s0_, s1_=s1_, s2_=s2_, s3_=s3_: e.tensor_scalar(s2_, s1_, 1.0, -1.0, ALU.add, ALU.add), d3, wpb)
                    d5 = ac(lambda e, s0_=s0_, s1_=s1_, s2_=s2_, s3_=s3_: e.activation(s3_, s1_, ACT.Ln, bias=1.0), d3, wpb)
                    d6 = po(lambda e, s0_=s0_, s1_=s1_, s2_=s2_, s3_=s3_: e.tensor_tensor(s2_, s1_, s2_, ALU.subtract), d4)
                    d7 = po(lambda e, s0_=s0_, s1_=s1_, s2_=s2_, s3_=s3_: e.tensor_tensor(s3_, s3_, s2_, ALU.add), d5, d6)
                    d8 = po(lambda e, s0_=s0_, s1_=s1_, s2_=s2_, s3_=s3_, eb=eb, hs=hs: e.tensor_tensor(dtb[:, eb, hs], s3_, s0_, ALU.add), d7, d1, S["dt"])
                    d9 = po(lambda e, s0_=s0_, s1_=s1_, s2_=s2_, s3_=s3_, eb=eb, hs=hs: e.tensor_tensor(dtu[:, eb, hs], dtb[:, eb, hs], u2[:, eb, hs], ALU.mult), d8, uu)
                    dA.free(ja, d8)
                    G.free(jb, d8)
                    dtd.append(d8)
                    dud.append(d9)
                    yield
                G.free(jr, t, c4, c5, c6)
            xs, alls = [], []
            ylast = S["y"]
            for h in range(2):
                hs = slice(512 * h, 512 * h + 512)
                yt = [None, None]
                for n in range(NS):
                    tb = pe(lambda e, n=n, hs=hs: e.matmul(BB[:, :], idm[:, n:n + 1].to_broadcast((96, 128)), BC[:, hs], start=True, stop=True), bc, c_sel, S["bb"])
                    ig, gb, wg = G.take()
                    v1 = dv(lambda e, gb=gb, hs=hs: e.tensor_tensor(gb[:, :, :], BB[:, :].unsqueeze(1).to_broadcast((128, 2, 512)),
                                                                   dtu[:, :, hs], ALU.mult), tb, dud, wg)
                    S["bb"] = [v1]
                    ia, da, wa = dA.take()
                    es = [ac(lambda e, eb=eb, n=n, da=da, hs=hs: e.activation(da[:, eb, :], dtb[:, eb, hs], ACT.Exp, scale=An[:, eb, n:n + 1]),
                             dtd, c_an, wa) for eb in range(2)]
                    sc = [dv(lambda e, eb=eb, n=n, da=da, gb=gb, h=h: e.tensor_tensor_scan(
                        gb[:, eb, :], da[:, eb, :], gb[:, eb, :], 0.0 if h == 0 else hl[:, eb, n:n + 1], ALU.mult, ALU.add),
                        es[eb], v1, S["hl"] if h else None) for eb in range(2)]
                    dA.free(ia, *sc)
                    v3 = None
                    if h == 0:
                        v3 = dv(lambda e, n=n, gb=gb: e.tensor_copy(hl[:, :, n:n + 1], gb[:, :, 511:512]), sc, S["hl"], c_z)
                        alls.append(v3)
                    tcb = pe(lambda e, n=n, hs=hs: e.matmul(CB[:, :], idm[:, 16 + n:17 + n].to_broadcast((96, 128)), BC[:, hs],
                                                            start=True, stop=True), bc, S["cb"])
                    v2 = dv(lambda e, gb=gb: e.tensor_tensor(gb[:, :, :], CB[:, :].unsqueeze(1).to_broadcast((128, 2, 512)),
                                                            gb[:, :, :], ALU.mult), tcb, sc, v3)
                    S["cb"] = [v2]
                    for eb in range(2):
                        yt[eb] = pe(lambda e, eb=eb, n=n, gb=gb: e.matmul(Y[eb][:, :], ident, gb[:, eb, :], start=(n == 0), stop=(n == NS - 1)),
                                    v2, ylast)
                    G.free(ig, yt[1])
                    yield
                if h == 0:
                    S["hl"] = alls
                jy, yg, wy = G.take()
                ys = [dv(lambda e, eb=eb, hs=hs, yg=yg: e.scalar_tensor_tensor(yg[:, eb, :], u2[:, eb, hs], Dp[:, eb:eb + 1], Y[eb][:, :],
                                                                              ALU.mult, ALU.add), yt[1], wy, l_v) for eb in range(2)]
                ylast = ys
                gt = po(lambda e, hs=hs, yg=yg: e.tensor_tensor(yg[:, :, :], yg[:, :, :], zs[:, :, hs], ALU.mult), ys, zz)
                i, bank, w = PS.take()
                for k in range(4):
                    for eb in range(2):
                        t = pe(lambda e, k=k, eb=eb, bank=bank, yg=yg: e.matmul(
                            bank[:, 128 * k:128 * k + 128], yg[:, eb, 128 * k:128 * k + 128],
                            Wout[:, eb, :], start=(eb == 0), stop=(eb == 1)), gt, l_wo, w)
                G.free(jy, t)
                xv = X[:, 8 * b + 4 * h:8 * b + 4 * h + 4, :].rearrange("p a c -> p (a c)")
                x1 = dv(lambda e, xv=xv, bank=bank, h=h: e.scalar_tensor_tensor(
                    xv, bank[:, :], res, xv, ALU.mult, ALU.add), t, xa, no, l_res)
                PS.free(i, x1)
                xs.append(x1)
                yield
            S["y"] = ylast
            S["zs"] = [gt]
            S["u2"] = [gt] + ys
            S["dt"] = sc + [v1]
            S["BC"] = [tcb]
            S["hl"] = sc
            xready[b] = xs

        outs = []

        def store(b):
            outs.append(dma(lambda e: e.dma_start(out[b].rearrange("(i p) c -> p i c", p=128), X[:, 8 * b:8 * b + 8, :]), xready[b]))

        def chain(*gens):
            for g in gens:
                yield from g()

        def run(g):
            for _ in g:
                pass

        def beside(main, side):
            ms, ss = main, side
            alive = True
            for _ in ms:
                for _ in range(SIDE_STEPS[0]):
                    if alive:
                        alive = next(ss, "end") != "end"
            for _ in ss:
                pass

        def final(b):
            yield from ffn(b)
            store(b)

        run(attention(0))
        run(ffn(0))
        for b in range(NB):
            side = []
            if b:
                side.append(lambda b=b: final(b - 1))
            if b + 1 < NB:
                side.append(lambda b=b: attention(b + 1))
                side.append(lambda b=b: ffn(b + 1))
            beside(mamba(b), chain(*side))
        run(final(NB - 1))

        sems = {e: ctx.enter_context(nc.semaphore(f"s_{e}")) for e in Queue.ENGINES}
        count = [0]

        def new_sem():
            count[0] += 1
            return ctx.enter_context(nc.semaphore(f"s_dma{count[0]}"))

        q.number(sems, new_sem)
        block = ctx.enter_context(nc.Block())

        @block.sync
        def _(eng):
            q.write("sync", eng)
            for t in outs:
                eng.wait_ge(t.sem, 16)

        @block.tensor
        def _(eng):
            q.write("tensor", eng)

        @block.vector
        def _(eng):
            q.write("vector", eng)

        @block.scalar
        def _(eng):
            q.write("scalar", eng)

        @block.gpsimd
        def _(eng):
            q.write("gpsimd", eng)


SIDE_STEPS = [1]

_INS = {"x": "L0_attn_a_x", "Wq": "L0_attn_a_Wq", "Wk": "L0_attn_a_Wk", "Wv": "L0_attn_a_Wv", "Wo": "L0_attn_a_Wo",
        "ln_g": "L0_attn_b_ln_g", "ln_b": "L0_attn_b_ln_b", "W_in": "L0_attn_b_W_in", "conv_w": "L0_attn_b_conv_w",
        "conv_b": "L0_attn_b_conv_b", "W_xp": "L0_attn_b_W_xp", "W_dt": "L0_attn_b_W_dt", "b_dt": "L0_attn_b_b_dt",
        "A_log": "L0_attn_b_A_log", "D_param": "L0_attn_b_D_param", "W_out": "L0_attn_b_W_out", "res": "L0_attn_b_res_scale",
        "k0": "L0_ffn_k0", "k1": "L0_ffn_k1", "k2": "L0_ffn_k2", "s0": "L0_ffn_s0", "s1": "L0_ffn_s1", "s2": "L0_ffn_s2"}


def kernel(**inputs):
    import numpy as _np
    import concourse.bacc as _bacc
    from concourse import mybir as _mybir
    from concourse.bass_utils import run_bass_kernel_spmd as _run

    nc = _bacc.Bacc("TRN2", target_bir_lowering=False, num_devices=1)
    arrays, args = {}, {}
    for short, name in _INS.items():
        a = _np.ascontiguousarray(inputs[name])
        if short in ("s0", "s1", "s2", "res"):
            a = a.reshape(1, 1)
        arrays[f"in_{short}"] = a
        args[short] = nc.dram_tensor(f"in_{short}", a.shape, _mybir.dt.from_np(a.dtype), kind="ExternalInput").ap()
    c = constants()
    arrays["in_consts"] = c
    args["consts"] = nc.dram_tensor("in_consts", c.shape, _mybir.dt.from_np(c.dtype), kind="ExternalInput").ap()
    o = nc.dram_tensor("out_0", (NB, T, C), _mybir.dt.float32, kind="ExternalOutput").ap()
    hybrid_block(nc, args, o)
    r = _run(nc, [arrays], core_ids=[0])
    return r.results[0]["out_0"]
```

```python
from contextlib import ExitStack

import numpy as np

import concourse.bass as bass
from concourse import mybir

F32 = mybir.dt.float32
BF16 = mybir.dt.bfloat16
F16 = mybir.dt.float16
U8 = mybir.dt.uint8
ALU = mybir.AluOpType
ACT = mybir.ActivationFunctionType
AX = mybir.AxisListType

NB, T, C, NH, HD = 4, 1024, 128, 16, 8
E2, NS, KC, RK = 2, 16, 4, 8
EPS = 1e-5
NEG = -1e30

CONST = {}
_at = 0
for _name, _n in (("ident", 128), ("e4", 128), ("e32", 32), ("hmask", 4), ("qmask", 4), ("idmod", 32), ("hsel", 128)):
    CONST[_name] = (_at, _n)
    _at += _n
NCONST = _at
NMASK = 3 * 512


def constants():
    out = np.zeros((128, NCONST + NMASK), np.float32)

    def put(name, a):
        at, n = CONST[name]
        out[: a.shape[0], at:at + n] = a.reshape(a.shape[0], n)

    p = np.arange(128)
    put("ident", np.eye(128, dtype=np.float32))
    q, k = np.arange(32)[:, None], np.arange(64)[None, :]
    win = np.where((k <= q + 32) & (k >= q + 1), 0.0, NEG)
    first = np.where((k <= q + 32) & (k >= q + 1) & (k >= 32), 0.0, NEG)
    r, c = np.arange(32)[:, None], np.arange(32)[None, :]
    stride = np.where((r // 16 == c // 16) & (c % 16 < r % 16), 0.0, NEG)
    head = np.concatenate([first] + [win] * 7, 1)
    rest = np.concatenate([win] * 8, 1)
    far = np.concatenate([stride] * 16, 1)
    out[:, NCONST:] = np.tile(np.concatenate([head, rest, far], 1), (4, 1))
    put("e4", (p[:, None] % 32 == p[None, :] % 32).astype(np.float32))
    put("e32", (p[:, None] % 32 == np.arange(32)[None, :]).astype(np.float32))
    put("hmask", (p[:, None] // 32 == np.arange(4)[None, :]).astype(np.float32))
    put("qmask", ((p[:, None] // 8 % 4 == np.arange(4)[None, :]) * float(HD) ** -0.5).astype(np.float32))
    put("idmod", (p[:96, None] % 32 == np.arange(32)[None, :]).astype(np.float32))
    put("hsel", (np.arange(16)[:, None] == p[None, :] // 8).astype(np.float32))
    return out


class Tok:

    def __init__(self, eng):
        self.eng, self.used, self.sem, self.value = eng, False, None, 0


def size(ap):
    n = 1
    for d in ap.shape[1:]:
        n *= d
    return n


class Costs:

    def __init__(self, name):
        self.name = name

    def plain(self, out, *_, **k):
        per, base = {"vector": (1.04, 60), "scalar": (0.84, 90), "gpsimd": (1.0, 100)}[self.name]
        return base + per * size(out)

    tensor_copy = tensor_scalar = scalar_tensor_tensor = tensor_tensor_scan = copy = activation = memset = bn_aggr = plain

    def bn_stats(self, out, in_):
        return self.plain(in_)

    def tensor_reduce(self, out, in_, *_):
        return self.plain(in_)

    def reciprocal(self, out, in_):
        return 60 + 6.3 * size(out)

    def tensor_tensor(self, out, a, b, op):
        if self.name == "gpsimd":
            return 100 + (169 if op == ALU.pow else 2.25) * size(out)
        return self.plain(out)

    def matmul(self, out, lhsT, rhs, **k):
        return max(64, size(rhs)) / 2.4 * (4 if rhs.dtype == F32 else 1)

    def transpose(self, out, in_, ident):
        return 54

    def dma_start(self, *_, **k):
        return 2000

    def preload_act_table_set(self, *_):
        return 1300


class Queue:

    ENGINES = ("tensor", "vector", "scalar", "gpsimd", "sync")
    AFTER = {"tensor": 200, "vector": 80, "scalar": 120, "gpsimd": 100, "sync": 0}

    def __init__(self):
        self.streams, self.now = {}, None
        self.ops = {e: [] for e in self.ENGINES}
        self.costs = {e: Costs(e) for e in self.ENGINES}

    def stream(self, name):
        self.now = self.streams.setdefault(name, {e: [] for e in self.ENGINES})

    def add(self, eng, fn, waits, dma=False):
        tok = Tok(eng)
        tok.dma = dma
        flat, stack = [], [waits]
        while stack:
            w = stack.pop()
            if isinstance(w, Tok):
                w.used = True
                flat.append(w)
            elif w is not None:
                stack.extend(w)
        self.now[eng].append((flat, fn, tok, fn(self.costs[eng])))
        return tok

    def merge(self):
        free = {e: 0.0 for e in self.ENGINES}
        done = {}
        at = {(s, e): 0 for s in self.streams for e in self.ENGINES}
        left = sum(len(x) for v in self.streams.values() for x in v.values())
        while left:
            best = None
            for e in self.ENGINES:
                for rank, s in enumerate(self.streams):
                    ops = self.streams[s][e]
                    if at[s, e] >= len(ops):
                        continue
                    flat, _, tok, cost = ops[at[s, e]]
                    start = free[e]
                    for w in flat:
                        if w not in done:
                            break
                        start = max(start, done[w])
                    else:
                        if best is None or (start, rank) < best[:2]:
                            best = (start, rank, s, e)
            start, _, s, e = best
            flat, fn, tok, cost = self.streams[s][e][at[s, e]]
            at[s, e] += 1
            free[e] = start + cost
            done[tok] = start + cost + self.AFTER[e]
            if e == "sync":
                free[e] = start + 60
            self.ops[e].append((flat, fn, tok))
            left -= 1

    def number(self, sem_of_engine, new_sem):
        for e, ops in self.ops.items():
            n = 0
            for _, _, tok in ops:
                if tok.dma:
                    tok.sem, tok.value = new_sem(), 16
                elif tok.used:
                    n += 1
                    tok.sem, tok.value = sem_of_engine[e], n

    def write(self, name, eng):
        seen = {}
        for waits, fn, tok in self.ops[name]:
            need = {}
            for w in waits:
                k = id(w.sem)
                if k not in need or need[k].value < w.value:
                    need[k] = w
            for k, w in need.items():
                if seen.get(k, 0) < w.value:
                    eng.wait_ge(w.sem, w.value)
                    seen[k] = w.value
            ins = fn(eng)
            if tok.dma:
                ins.then_inc(tok.sem, 16)
            elif tok.used:
                ins.then_inc(tok.sem, 1)


class Slots:

    def __init__(self, bufs):
        self.bufs, self.n, self.last, self.held = bufs, 0, [[] for _ in bufs], set()

    def take(self):
        i = self.n % len(self.bufs)
        self.n += 1
        assert i not in self.held
        self.held.add(i)
        w, self.last[i] = self.last[i], []
        return i, self.bufs[i], w

    def free(self, i, *toks):
        self.held.discard(i)
        self.last[i].extend(toks)


def hybrid_block(nc, ins, out):
    ctx = ExitStack()
    with ctx:
        def sb(name, shape, dt=F32):
            return ctx.enter_context(nc.sbuf_tensor(name, shape, dt))

        q = Queue()
        for name in STREAMS:
            q.stream(name)
        q.stream("weights")

        def pe(fn, *w):
            return q.add("tensor", fn, w)

        def dv(fn, *w):
            return q.add("vector", fn, w)

        def ac(fn, *w):
            return q.add("scalar", fn, w)

        def po(fn, *w):
            return q.add("gpsimd", fn, w)

        def dma(fn, *w):
            return q.add("sync", fn, w, dma=True)

        banks = [ctx.enter_context(nc.psum_tensor(f"ps{i}", [128, 512], F32)) for i in range(8)]
        PA, PF, PM = Slots(banks[0:3]), Slots(banks[3:4]), Slots(banks[4:8])

        cst = sb("cst", [128, NCONST])

        def const(name, rows=128):
            at, n = CONST[name]
            return cst[0:rows, at:at + n]

        ident = const("ident")
        hmask = const("hmask")
        e32 = const("e32")
        masks = sb("masks", [128, 3, 512], BF16)
        e4 = sb("e4", [128, 128], BF16)
        idm = sb("idm", [96, 32], BF16)
        X = sb("X", [128, NB * 8, C])
        WT = sb("WT", [128, 4, 128])
        Win = sb("Win", [128, 512])
        Wk = sb("Wk", [128, KC, 256])
        Wxr = sb("Wxr", [128, 2, 40])
        Wx = sb("Wx", [128, 2, 104])
        Wdt = sb("Wdt", [128, 256])
        Wout = sb("Wout", [128, 2, 128])
        Al = sb("Al", [128, 2, NS])
        Ap = sb("Ap", [128, 2, NS])
        An = sb("An", [128, 2, NS])
        vec = sb("vec", [128, 16])
        bdt, cvb, Dp = vec[:, 0:2], vec[:, 2:4], vec[:, 4:6]
        lng, lnb, res = vec[:, 6:7], vec[:, 7:8], vec[:, 8:9]
        s3 = vec[:, 9:12]
        sgn = sb("sgn", [128, 8])
        fsc = sb("fsc", [128, 4])
        expo = sb("expo", [128, 8])
        w0 = sb("w0", [128, 512], F16)
        w1 = sb("w1", [128, 4, 512], F16)
        w2 = sb("w2", [128, 4, 128], F16)

        G = Slots([sb(f"g{i}", [128, 2, 512]) for i in range(4)])
        dA = Slots([sb(f"dA{i}", [128, 2, 512]) for i in range(2)])

        def flat(t):
            return t[:, :, :].rearrange("p a n -> p (a n)")

        mraw0, mraw1 = flat(G.bufs[0]), flat(G.bufs[1])
        cwr = flat(G.bufs[2])
        kraw = flat(G.bufs[3]).bitcast(U8)
        k0r = kraw[:, 0:1024].rearrange("p (a n) -> p a n", a=2)
        k1r = kraw[:, 1024:3072].rearrange("p (a n) -> p a n", a=4)
        k2r = kraw[:, 3072:3584].rearrange("p (a n) -> p a n", a=4)
        Wraw = flat(dA.bufs[0])[:, 0:512].rearrange("p (a n) -> p a n", a=4)
        kt = flat(dA.bufs[1])[:, 0:512]

        def load(dst, src):
            def go(e):
                with nc.allow_non_contiguous_dma(reason="small vectors"):
                    return e.dma_start(dst, src)
            return dma(go)

        l_x = [None] * NB

        def load_x(b):
            l_x[b] = load(X[:, 8 * b:8 * b + 8, :], ins["x"][b].rearrange("(i p) c -> p i c", p=128))

        load_x(0)
        l_cst = load(cst[:, :], ins["consts"][:, 0:NCONST])
        l_m = [load(mraw0, ins["consts"][:, NCONST:NCONST + 1024]), load(mraw1[:, 0:512], ins["consts"][:, NCONST + 1024:])]
        l_w = [load(Wraw[:, i, :], ins[n]) for i, n in enumerate(("Wq", "Wk", "Wv", "Wo"))]
        l_s = [load(vec[:, 9 + i:10 + i], ins[f"s{i}"].to_broadcast((128, 1))) for i in range(3)]
        l_k0 = load(k0r, ins["k0"].rearrange("(a p) n -> p a n", p=128))
        l_k1 = load(k1r, ins["k1"].rearrange("(a p) n -> p a n", p=128))
        l_k2 = load(k2r, ins["k2"].rearrange("(a p) n -> p a n", p=128))
        l_win = load(Win[:, :], ins["W_in"])
        l_cw = load(cwr, ins["conv_w"].rearrange("(o e) k -> o (e k)", o=1).to_broadcast((128, 256 * KC)))
        l_wx = load(Wxr[:, :, :], ins["W_xp"].rearrange("(a p) n -> p a n", p=128))
        l_wdt = load(Wdt[96:104, :], ins["W_dt"])
        l_wo = load(Wout[:, :, :], ins["W_out"].rearrange("(a p) n -> p a n", p=128))
        l_al = load(Al[:, :, :], ins["A_log"].rearrange("(a p) n -> p a n", p=128))
        l_v = [load(vec[:, 2 * i:2 * i + 2], ins[n].rearrange("(a p) -> p a", p=128))
               for i, n in enumerate(("b_dt", "conv_b", "D_param"))]
        l_v += [load(vec[:, 6 + i:7 + i], ins[n].rearrange("(p o) -> p o", o=1)) for i, n in enumerate(("ln_g", "ln_b"))]
        l_res = load(vec[:, 8:9], ins["res"].to_broadcast((128, 1)))
        for b in range(1, NB):
            load_x(b)

        mk_ = masks[:, :, :].rearrange("p a n -> p (a n)")
        c_mask = [dv(lambda e: e.tensor_copy(mk_[:, 0:1024], mraw0), l_m[0]), dv(lambda e: e.tensor_copy(mk_[:, 1024:1536], mraw1[:, 0:512]), l_m[1])]
        c_e4 = po(lambda e: e.tensor_scalar(e4[:, :], const("e4"), 1.0, None, ALU.mult), l_cst)
        c_sel = dv(lambda e: e.tensor_copy(idm[:, :], const("idmod", 96)), l_cst)
        c_expo = po(lambda e: e.memset(expo[:, :], -0.5))
        i, bank, w = PA.take()
        for j in range(4):
            t_w = pe(lambda e, j=j, bank=bank: e.transpose(bank[:, 128 * j:128 * j + 128], Wraw[:, j, :], ident), l_w[j], l_cst, w)
        c_wt = ac(lambda e, bank=bank: e.copy(WT[:, :, :].rearrange("p a n -> p (a n)"), bank[:, :]), t_w)
        PA.free(i, c_wt)
        dA.free(0, t_w)

        g1 = dv(lambda e: e.tensor_scalar(sgn[:, 0:3], s3, 0.0, None, ALU.is_gt), l_s)
        g2 = dv(lambda e: e.tensor_scalar(sgn[:, 3:6], s3, 0.0, None, ALU.is_lt), l_s)
        g3 = dv(lambda e: e.tensor_tensor(sgn[:, 0:3], sgn[:, 0:3], sgn[:, 3:6], ALU.subtract), g1, g2)
        g4 = dv(lambda e: e.tensor_tensor(fsc[:, 0:3], sgn[:, 0:3], s3, ALU.mult), g3)
        g5 = dv(lambda e: e.tensor_tensor(fsc[:, 3:4], fsc[:, 0:1], fsc[:, 1:2], ALU.mult), g4)
        c_f = dv(lambda e: e.tensor_scalar(fsc[:, 3:4], fsc[:, 3:4], s3[:, 2:3], 64.0, ALU.mult, ALU.mult), g5)
        FS = fsc[:, 3:4]
        g6 = dv(lambda e: e.tensor_scalar(sgn[:, 3:5], sgn[:, 0:2], 2.0, None, ALU.mult), g3)
        g7 = dv(lambda e: e.tensor_scalar(sgn[:, 4:5], sgn[:, 1:2], 0.125, None, ALU.mult), g6)
        g8 = dv(lambda e: e.tensor_tensor(kt, k0r[:, 0, :], k0r[:, 1, :], ALU.subtract), l_k0)
        c_w0 = dv(lambda e: e.tensor_scalar(w0[:, :], kt, sgn[:, 3:4], None, ALU.mult), g8, g6)
        c_w1 = dv(lambda e: e.tensor_scalar(w1[:, :, :].rearrange("p a n -> p (a n)"), kraw[:, 1024:3072],
                                            0.5, sgn[:, 4:5], ALU.subtract, ALU.mult), g7, l_k1)
        c_w2 = dv(lambda e: e.tensor_scalar(w2[:, :, :].rearrange("p a n -> p (a n)"), kraw[:, 3072:3584],
                                            2.0, 1.0, ALU.mult, ALU.subtract), l_k2)

        cwv = cwr.rearrange("p (e k) -> p k e", k=KC)
        c_wk = dv(lambda e: e.tensor_tensor(Wk[:, :, :], cwv, Win[:, 0:256].unsqueeze(1).to_broadcast((128, KC, 256)), ALU.mult),
                  l_win, l_cw)
        G.free(0, c_mask)
        G.free(1, c_mask)
        G.free(2, c_wk)
        G.free(3, c_w0, c_w1, c_w2)
        dA.free(1, c_w0)
        wx = [dv(lambda e, r=r: e.tensor_copy(Wx[:, :, 32 * r:32 * r + 32], Wxr[:, :, 8:40]), l_wx) for r in range(3)]
        wx.append(dv(lambda e: e.tensor_copy(Wx[:, :, 96:104], Wxr[:, :, 0:8]), l_wx))
        a1 = ac(lambda e: e.activation(Ap[:, :, :], Al[:, :, :], ACT.Exp), l_al)
        c_an = dv(lambda e: e.tensor_scalar(An[:, :, :], Ap[:, :, :], -1.0, None, ALU.mult), a1)

        xready = [[l_x[b]] for b in range(NB)]

        small = {n: [Slots([sb(f"{n}{k}", [128] + d)]) for k, d in (("st", [8, 6]), ("mv", [8, 2]), ("rs", [2, 8]))]
                 for n in STREAMS}
        LNA = Slots([sb("lna", [128, 8, C])])
        LNF = Slots([sb("lnf", [128, 4, C])])
        LNM = Slots([sb("lnm", [128, 8, C])])

        aT = sb("aT", [128, 32 + T])
        KT = sb("KT", [128, 32 + T])
        aP = sb("aP", [128, T])
        QT = sb("QT", [128, T])
        QM = Slots([sb(f"qm{i}", [128, 8, 4, 32]) for i in range(2)])
        V1 = Slots([sb("v1", [128, 4, 2, 4, 33])])
        V2 = Slots([sb("v2", [128, 4, 4, 4, 33])])
        Sx = Slots([sb(f"sx{i}", [128, 512]) for i in range(2)])
        PT = Slots([sb(f"pt{i}", [128, 4, 128]) for i in range(2)])
        mx = Slots([sb(f"mx{i}", [128, 16]) for i in range(4)])
        OM = Slots([sb(f"om{i}", [128, 16, 4, 32]) for i in range(1)])
        LM = Slots([sb(f"lm{i}", [128, 2, 16, 4, 4]) for i in range(1)])
        far = sb("far", [128, T])
        farc = sb("farc", [16, 2, T])
        near = Slots([sb(f"near{i}", [128, 256]) for i in range(1)])
        nearc = Slots([sb(f"nearc{i}", [16, 2, 256]) for i in range(1)])
        tmp = sb("tmp", [128, 2, 256])
        tmc = sb("tmc", [16, 4, 256])

        FA = Slots([sb(f"fa{i}", [128, 2, 512], F16) for i in range(1)])
        H0 = Slots([sb(f"h0{i}", [128, 2, 4, 512], F16) for i in range(1)])
        H1 = Slots([sb(f"h1{i}", [128, 2, 4, 512], F16) for i in range(1)])

        xnT = sb("xnT", [128, 4 + T])
        zs = sb("zs", [128, 2, T])
        u2 = sb("u2", [128, 2, T])
        dtb = sb("dtb", [128, 2, T])
        dtu = sb("dtu", [128, 2, T])
        BC = sb("BC", [96, T], BF16)
        hl = sb("hl", [128, 2, NS])

        z = [po(lambda e: e.memset(aT[:, 0:32], 0.0)), po(lambda e: e.memset(KT[:, 0:32], 0.0)),
             po(lambda e: e.memset(xnT[:, 0:4], 0.0)), po(lambda e: e.memset(hl[:, :, :], 0.0))]
        ones = []
        for v, n in ((V1.bufs[0], 2), (V2.bufs[0], 4)):
            zv = po(lambda e, v=v: e.memset(v[:, :, :, :, :], 0.0))
            r = 128 // n
            ones += [dv(lambda e, k=k, v=v, r=r: e.memset(v[r * k:r * k + r, :, k, :, 32], 1.0), zv) for k in range(n)]
        c_z = z + ones

        def norm(name, src, n, ready, dst, dwait):
            st, mv, rs = small[name]
            i1, s_, w1_ = st.take()
            i2, m_, w2_ = mv.take()
            i3, r_, w3_ = rs.take()
            ag = []
            ss = [dv(lambda e, k=k: e.bn_stats(s_[:, k, :], src(k)), ready, w1_) for k in range(n)]
            for k in range(n):
                ag.append(dv(lambda e, k=k: e.bn_aggr(m_[:, k, :], s_[:, k, :]), ss[k], w2_))
            st.free(i1, *ag)
            a = po(lambda e: e.tensor_scalar(r_[:, 1, 0:n], m_[:, 0:n, 1], 1.0, EPS, ALU.mult, ALU.add), ag, w3_)
            p = po(lambda e: e.tensor_tensor(r_[:, 0, 0:n], r_[:, 1, 0:n], expo[:, 0:n], ALU.pow), a, c_expo)
            m1 = po(lambda e: e.tensor_tensor(r_[:, 1, 0:n], m_[:, 0:n, 0], r_[:, 0, 0:n], ALU.mult), p)
            m2 = po(lambda e: e.tensor_scalar(r_[:, 1, 0:n], r_[:, 1, 0:n], -1.0, 0.0, ALU.mult, ALU.add), m1)
            mv.free(i2, m1)
            o = [po(lambda e, k=k: e.tensor_scalar(dst[:, k, :], src(k), r_[:, 0, k:k + 1], r_[:, 1, k:k + 1], ALU.mult, ALU.add),
                    m2, ready, dwait) for k in range(n)]
            rs.free(i3, *o)
            return o

        state = {"attn_in": [], "attn_v": [], "olm": [], "qk": [], "tmp": [], "xnT": [], "XA": [], "zs": [], "u2": [],
                 "dt": [], "BC": [], "y": [], "bb": [], "cb": [], "hl": [], "yg": [], "dlo": [], "Hs": [], "Ms": [], "Rs": [], "sp": [[], [], [], []]}

        def attention(b):
            q.stream("attention")
            S = state
            il, A, wl = LNA.take()
            no = norm("attention", lambda k: X[:, 8 * b + k, :], 8, xready[b], A, wl)
            tr, cp = [], []
            for h in range(2):
                i, bank, w = PA.take()
                for k in range(4):
                    t = pe(lambda e, k=k, h=h, bank=bank: e.transpose(bank[:, 128 * k:128 * k + 128], A[:, 4 * h + k, :], ident),
                           no[4 * h + k], w, l_cst)
                    tr.append(t)
                c = ac(lambda e, h=h, bank=bank: e.copy(aT[:, 32 + 512 * h:32 + 512 * h + 512], bank[:, :]), t, S["attn_in"], c_z)
                cp.append(c)
                PA.free(i, c)
            aPd = [po(lambda e, g=g: e.tensor_scalar(
                aP[:, 512 * g:512 * g + 512].rearrange("p (r j) -> p r j", j=16),
                aT[:, 32:32 + T].rearrange("p (j r) -> p r j", r=64)[:, 32 * g:32 * g + 32, :], 1.0, 0.0, ALU.mult, ALU.add),
                cp, S["attn_in"]) for g in range(2)]
            LNA.free(il, *tr)
            qk_done, q_done, k_done = [], [], []
            for h in range(2):
                i, bank, w = PA.take()
                t = pe(lambda e, h=h, bank=bank: e.matmul(bank[:, :], WT[:, 0, :], aT[:, 32 + 512 * h:544 + 512 * h], start=True, stop=True),
                       c_wt, cp, w)
                qk_done.append(t)
                c = ac(lambda e, h=h, bank=bank: e.copy(QT[:, 512 * h:512 * h + 512], bank[:, :]), t, S["qk"])
                q_done.append(c)
                PA.free(i, c)
                i, bank, w = PA.take()
                t = pe(lambda e, h=h, bank=bank: e.matmul(bank[:, :], WT[:, 1, :], aT[:, 32 + 512 * h:544 + 512 * h], start=True, stop=True), w)
                qk_done.append(t)
                c = ac(lambda e, h=h, bank=bank: e.copy(KT[:, 32 + 512 * h:544 + 512 * h], bank[:, :]), t, S["qk"], c_z)
                k_done.append(c)
                PA.free(i, c)
            aw = aT[:, :]

            def values(kind, g, cp=cp):
                i, bank, w = PA.take()
                iv, V, wv = (V1, V2)[kind].take()
                for k in range(4):
                    m = 4 * g + k
                    if kind:
                        t = pe(lambda e, k=k, m=m, bank=bank: e.matmul(
                            bank[:, 128 * k:128 * k + 128], aP[:, 128 * m:128 * m + 128], WT[:, 2, :], start=True, stop=True), aPd, w)
                        continue
                    for s in range(2):
                        t = pe(lambda e, k=k, m=m, s=s, bank=bank: e.matmul(
                            bank[64 * s:64 * s + 64, 128 * k:128 * k + 128],
                            aw[:, 64 * m + 32 * s:64 * m + 32 * s + 64], WT[:, 2, :], start=True, stop=True), cp, w)
                qk_done.append(t)
                r = (64, 32)[kind]
                vs = [ac(lambda e, s=s: e.copy(V[r * s:r * s + r, :, s, :, 0:32],
                                               bank[r * s:r * s + r, :].rearrange("p (k a d) -> p k a d", k=4, a=4)), t, wv, c_z)
                      for s in range(128 // r)]
                PA.free(i, *vs)
                return iv, V, vs

            Qs = QT[:, :].rearrange("p (j r) -> p r j", r=64)
            qmask = const("qmask")
            Ks = KT[:, 32:32 + T].rearrange("p (j r) -> p r j", r=64)
            s_last, farm, merged, atts, q_read = [], [], [], [], []
            for kind in (1, 0):
                nq, kw, nw = ((8, 64, 2), (16, 32, 4))[kind]
                for g in range((4, 2)[kind]):
                    io, om, wo_ = OM.take()
                    im, lm, wm_ = LM.take()
                    iv, V, v_done = values(kind, g)
                    qm, qm_done = [], []
                    for s in range(nq // 8):
                        iq, qt, wq = QM.take()
                        at = nq * g + 8 * s
                        qm.append((iq, qt))
                        for j in range(4):
                            if kind:
                                src = Qs[:, 2 * at:2 * at + 16, :].rearrange("p (a r) j -> p a r j", r=2)
                                dst = qt[:, :, j, :].rearrange("p a (r j) -> p a r j", r=2)
                            else:
                                src = QT[:, 32 * at:32 * at + 256].rearrange("p (a n) -> p a n", n=32)
                                dst = qt[:, :, j, :]
                            qm_done.append(po(lambda e, src=src, dst=dst, j=j: e.tensor_scalar(dst, src, qmask[:, j:j + 1], 0.0, ALU.mult, ALU.add),
                                              q_done, wq, l_cst))
                    q_read += qm_done
                    packed = []
                    for hg in range(4):
                        r0 = 32 * hg
                        i, bank, w = PA.take()
                        mk = 2 if kind else (0 if g == 0 else 1)
                        pe(lambda e, r0=r0, mk=mk, bank=bank: e.matmul(bank[:, :], e4[r0:r0 + 32, :], masks[r0:r0 + 32, mk, :], start=True,
                                                                      stop=False, skip_group_check=True), c_mask, c_e4, w)
                        for k in range(nq):
                            m = nq * g + k
                            lq = qm[k // 8][1][r0:r0 + 32, k % 8, :, :].rearrange("p a n -> p (a n)")
                            if kind == 0:
                                rk = KT[r0:r0 + 32, 32 * m:32 * m + 64]
                            else:
                                rk = Ks[r0:r0 + 32, 2 * m:2 * m + 2, :]
                            t = pe(lambda e, lq=lq, rk=rk, k=k, kw=kw, nq=nq, bank=bank: e.matmul(
                                bank[:, kw * k:kw * k + kw], lq, rk, start=False, stop=(k == nq - 1), skip_group_check=True), qm_done, k_done)
                        s_last.append(t)
                        ix, mm, wx_ = mx.take()
                        sv = bank[:, :].rearrange("p (a k) -> p a k", k=kw)
                        t = dv(lambda e, mm=mm, sv=sv, nq=nq: e.tensor_reduce(mm[:, 0:nq], sv, AX.X, ALU.max), t, wx_)
                        isx, sx, ws_ = Sx.take()
                        t2 = dv(lambda e, mm=mm, sv=sv, sx=sx, nq=nq, kw=kw: e.tensor_tensor(
                            sx[:, :].rearrange("p (a k) -> p a k", k=kw), sv, mm[:, 0:nq].unsqueeze(2).to_broadcast((128, nq, kw)),
                            ALU.subtract), t, ws_)
                        PA.free(i, t2)
                        pk = dv(lambda e, mm=mm, lm=lm, hg=hg, nq=nq: e.tensor_tensor(
                            lm[:, 1, 0:nq, hg, :], mm[:, 0:nq].unsqueeze(2).to_broadcast((128, nq, 4)),
                            hmask.unsqueeze(1).to_broadcast((128, nq, 4)), ALU.mult), t, wm_)
                        mx.free(ix, pk, t2)
                        packed.append(pk)
                        t3 = ac(lambda e, sx=sx: e.activation(sx[:, :], sx[:, :], ACT.Exp), t2)
                        i, bank, w = PA.take()
                        for k in range(4):
                            t4 = pe(lambda e, k=k, bank=bank, sx=sx: e.transpose(bank[:, 128 * k:128 * k + 128], sx[:, 128 * k:128 * k + 128], ident),
                                    t3, w)
                        Sx.free(isx, t4)
                        ip, pt, wp_ = PT.take()
                        t5 = ac(lambda e, pt=pt, bank=bank: e.copy(pt[:, :, :].rearrange("p a n -> p (a n)"), bank[:, :]), t4, wp_)
                        PA.free(i, t5)
                        per = (4, 2)[kind]
                        for o in range(4 // per):
                            i, bank, w = PA.take()
                            for k in range(per):
                                kk = per * o + k
                                t6 = pe(lambda e, k=k, kk=kk, bank=bank, pt=pt, g=g, hg=hg, nw=nw, V=V: e.matmul(
                                    bank[:, 33 * nw * k:33 * nw * (k + 1)], pt[:, kk, :], V[:, kk, :, hg, :], start=True, stop=True),
                                    t5, v_done, w)
                            ov = bank[:, 0:33 * nw * per].rearrange("p (a n) -> p a n", n=33)
                            a0, na = nw * per * o, nw * per
                            t7 = dv(lambda e, ov=ov, om=om, a0=a0, na=na, hg=hg: e.tensor_tensor(
                                om[:, a0:a0 + na, hg, :].rearrange("p a (h d) -> p a h d", h=4), ov[:, :, 0:32].rearrange("p a (h d) -> p a h d", h=4),
                                hmask.unsqueeze(1).unsqueeze(3).to_broadcast((128, na, 4, 8)), ALU.mult), t6, wo_)
                            t8 = dv(lambda e, ov=ov, lm=lm, a0=a0, na=na, hg=hg: e.tensor_tensor(
                                lm[:, 0, a0:a0 + na, hg, :], ov[:, :, 32:33].to_broadcast((128, na, 4)),
                                hmask.unsqueeze(1).to_broadcast((128, na, 4)), ALU.mult), t6, wm_)
                            PA.free(i, t7, t8)
                            packed += [t7, t8]
                        PT.free(ip, t6)
                    (V1, V2)[kind].free(iv, t6)
                    for iq, _ in qm:
                        QM.free(iq, s_last[-1])
                    done = []
                    for s in range(nq // 8):
                        i1, b1, wa = PA.take()
                        i2, b2, wb = PA.take()
                        for k in range(8):
                            a = 8 * s + k
                            t1 = pe(lambda e, k=k, a=a, b1=b1, om=om: e.matmul(
                                b1[:, 32 * k:32 * k + 32], om[:, a, :, :].rearrange("p a n -> p (a n)"), e32, start=True, stop=True), packed, wa)
                        for x in range(2):
                            for k in range(8):
                                a = 8 * s + k
                                t2 = pe(lambda e, k=k, a=a, x=x, b2=b2, lm=lm: e.matmul(
                                    b2[0:16, 256 * x + 32 * k:256 * x + 32 * k + 32], lm[:, x, a, :, :].rearrange("p a b -> p (a b)"),
                                    e32, start=True, stop=True), wb)
                        at = nq * g + 8 * s
                        if kind == 0:
                            olm = []
                            inr, nr, wn = near.take()
                            inc, nc_, wnc = nearc.take()
                            c1 = ac(lambda e, nr=nr, b1=b1: e.copy(nr[:, :], b1[:, 0:256]), t1, wn)
                            c2 = ac(lambda e, nc_=nc_, b2=b2: e.copy(nc_[:, :, :].rearrange("p a n -> p (a n)"), b2[0:16, :]), t2, wnc)
                            olm += [c1, c2]
                        else:
                            dst = far[:, :].rearrange("p (j r) -> p r j", r=64)[:, 2 * at:2 * at + 16, :]
                            v1 = b1[:, 0:256].rearrange("p (r j) -> p r j", j=16)
                            c1 = ac(lambda e, dst=dst, v1=v1: e.copy(dst, v1), t1, S["olm"])
                            dsc = farc[:, :, :].rearrange("p a (j r) -> p a r j", r=64)[:, :, 2 * at:2 * at + 16, :]
                            v2 = b2[0:16, :].rearrange("p (a r j) -> p a r j", a=2, j=16)
                            for x in range(2):
                                c2 = ac(lambda e, x=x, dsc=dsc, v2=v2: e.copy(dsc[:, x, :, :], v2[:, x, :, :]), t2, S["olm"])
                                farm.append(c2)
                            farm.append(c1)
                        PA.free(i1, c1)
                        PA.free(i2, c2)
                        done += [t1, t2]
                    OM.free(io, *done)
                    LM.free(im, *done)
                    if kind:
                        continue
                    cols = slice(256 * g, 256 * g + 256)
                    L1, M1 = nc_[:, 0, :], nc_[:, 1, :]
                    L2, M2 = farc[:, 0, cols], farc[:, 1, cols]
                    ta = dv(lambda e, M1=M1, M2=M2: e.tensor_tensor(tmc[:, 2, :], M1, M2, ALU.max), olm, farm, S["tmp"])
                    tb = po(lambda e, M1=M1: e.tensor_tensor(tmc[:, 0, :], M1, tmc[:, 2, :], ALU.subtract), ta)
                    tc_ = po(lambda e, M2=M2: e.tensor_tensor(tmc[:, 1, :], M2, tmc[:, 2, :], ALU.subtract), ta)
                    td = ac(lambda e: e.activation(tmc[:, 0:2, :], tmc[:, 0:2, :], ACT.Exp), tb, tc_)
                    f1 = po(lambda e, L1=L1: e.tensor_tensor(tmc[:, 2, :], L1, tmc[:, 0, :], ALU.mult), td)
                    f2 = po(lambda e, L2=L2: e.tensor_tensor(tmc[:, 3, :], L2, tmc[:, 1, :], ALU.mult), td)
                    f3 = po(lambda e: e.tensor_tensor(tmc[:, 2, :], tmc[:, 2, :], tmc[:, 3, :], ALU.add), f1, f2)
                    f4 = dv(lambda e: e.reciprocal(tmc[:, 2, :], tmc[:, 2, :]), f3)
                    f5 = po(lambda e: e.tensor_tensor(tmc[:, 0, :], tmc[:, 0, :], tmc[:, 2, :], ALU.mult), f4)
                    f6 = po(lambda e: e.tensor_tensor(tmc[:, 1, :], tmc[:, 1, :], tmc[:, 2, :], ALU.mult), f4)
                    nearc.free(inc, f1, ta, tb)
                    i, bank, w = PA.take()
                    f7 = pe(lambda e, bank=bank: e.matmul(bank[:, :], const("hsel", 16), tmc[:, 0:2, :], start=True, stop=True), f5, f6, w)
                    O2 = far[:, cols]
                    ATT = tmp[:, 0, :]
                    h1 = dv(lambda e, bank=bank, nr=nr: e.tensor_tensor(tmp[:, 0, :], bank[:, 0:256], nr[:, :], ALU.mult), f7)
                    h2 = dv(lambda e, bank=bank, O2=O2: e.tensor_tensor(tmp[:, 1, :], bank[:, 256:512], O2, ALU.mult), f7)
                    PA.free(i, h1, h2)
                    f8 = dv(lambda e: e.tensor_tensor(tmp[:, 0, :], tmp[:, 0, :], tmp[:, 1, :], ALU.add), h1, h2)
                    near.free(inr, h1)
                    merged += [h2, f2, ta, tc_]
                    i, bank, w = PA.take()
                    for k in range(2):
                        t = pe(lambda e, k=k, bank=bank: e.matmul(bank[:, 128 * k:128 * k + 128], ATT[:, 128 * k:128 * k + 128], WT[:, 3, :],
                                                                 start=True, stop=True), f8, w)
                    xv = X[:, 8 * b + 2 * g:8 * b + 2 * g + 2, :].rearrange("p a c -> p (a c)")
                    x1 = dv(lambda e, xv=xv, bank=bank: e.tensor_tensor(xv, bank[:, 0:256], xv, ALU.add), t, no)
                    PA.free(i, x1)
                    atts.append(x1)
                    S["tmp"] = [t, f7]
            S["attn_in"] = qk_done + aPd
            S["qk"] = s_last + q_read
            S["olm"] = merged
            xready[b] = atts

        def ffn(b):
            q.stream("ffn")
            xs = []
            for h in range(2):
                il, A, wl = LNF.take()
                no = norm("ffn", lambda k, h=h: X[:, 8 * b + 4 * h + k, :], 4, xready[b], A, wl)
                i, bank, w = PF.take()
                for k in range(4):
                    t = pe(lambda e, k=k, A=A, bank=bank: e.transpose(bank[:, 128 * k:128 * k + 128], A[:, k, :], ident),
                           no[k], w, l_cst)
                LNF.free(il, t)
                ia, fa, wa = FA.take()
                c1 = ac(lambda e, fa=fa, bank=bank: e.copy(fa[:, 0, :], bank[:, :]), t, wa)
                c2 = dv(lambda e, fa=fa, bank=bank: e.tensor_tensor(fa[:, 1, :], bank[:, :], fa[:, 0, :], ALU.subtract), c1, wa)
                PF.free(i, c2)
                ih, h0, wh = H0.take()
                r0 = []
                for mo in range(4):
                    i, bank, w = PF.take()
                    for s in range(2):
                        t = pe(lambda e, s=s, mo=mo, fa=fa, bank=bank: e.matmul(bank[:, :], w0[:, 128 * mo:128 * mo + 128], fa[:, s, :],
                                                                               start=(s == 0), stop=(s == 1)), c1, c2, c_w0, w)
                    e1 = ac(lambda e, mo=mo, h0=h0, bank=bank: e.activation(h0[:, 0, mo, :], bank[:, :], ACT.Relu), t, wh)
                    e2 = dv(lambda e, mo=mo, h0=h0, bank=bank: e.scalar_tensor_tensor(h0[:, 1, mo, :], bank[:, :], 0.0, h0[:, 0, mo, :],
                                                                                    ALU.max, ALU.subtract), e1, wh)
                    PF.free(i, e2)
                    r0.append(e2)
                FA.free(ia, t)
                i1, h1, wh1 = H1.take()
                r1 = []
                for mo in range(4):
                    i, bank, w = PF.take()
                    n = 0
                    for ki in range(4):
                        for s in range(2):
                            t = pe(lambda e, s=s, mo=mo, ki=ki, n=n, h0=h0, bank=bank: e.matmul(
                                bank[:, :], w1[:, ki, 128 * mo:128 * mo + 128], h0[:, s, ki, :], start=(n == 0), stop=(n == 7)), r0[ki], c_w1, w)
                            n += 1
                    e1 = ac(lambda e, mo=mo, h1=h1, bank=bank: e.activation(h1[:, 0, mo, :], bank[:, :], ACT.Relu), t, wh1)
                    e2 = dv(lambda e, mo=mo, h1=h1, bank=bank: e.scalar_tensor_tensor(h1[:, 1, mo, :], bank[:, :], 0.0, h1[:, 0, mo, :],
                                                                                    ALU.max, ALU.subtract), e1, wh1)
                    PF.free(i, e2)
                    r1.append(e2)
                H0.free(ih, t)
                i, bank, w = PF.take()
                for k in range(4):
                    n = 0
                    for ki in range(4):
                        for s in range(2):
                            t = pe(lambda e, s=s, k=k, ki=ki, n=n, h1=h1, bank=bank: e.matmul(
                                bank[:, 128 * k:128 * k + 128], h1[:, s, ki, 128 * k:128 * k + 128], w2[:, ki, :],
                                start=(n == 0), stop=(n == 7)), r1[ki], c_w2, w)
                            n += 1
                H1.free(i1, t)
                xv = X[:, 8 * b + 4 * h:8 * b + 4 * h + 4, :].rearrange("p a c -> p (a c)")
                x1 = dv(lambda e, xv=xv, bank=bank: e.scalar_tensor_tensor(xv, bank[:, :], FS, xv, ALU.mult, ALU.add), t, no, c_f)
                PF.free(i, x1)
                xs.append(x1)
            xready[b] = xs

        def mamba(b):
            q.stream("mamba")
            S = state
            il, A, wl = LNM.take()
            no = norm("mamba", lambda k: X[:, 8 * b + k, :], 8, xready[b], A, wl)
            Xf = X[:, 8 * b:8 * b + 8, :].rearrange("p a c -> p (a c)")
            xa = po(lambda e: e.tensor_tensor(Xf, Xf, A[:, :, :].rearrange("p a c -> p (a c)"), ALU.add), no)
            no2 = norm("mamba", lambda k: A[:, k, :], 8, no, A, xa)
            trs, cp = [], []
            for h in range(2):
                i, bank, w = PM.take()
                for k in range(4):
                    t = pe(lambda e, k=k, h=h, bank=bank: e.transpose(bank[:, 128 * k:128 * k + 128], A[:, 4 * h + k, :], ident),
                           no2[4 * h + k], w)
                trs.append(t)
                c = ac(lambda e, h=h, bank=bank: e.activation(xnT[:, 4 + 512 * h:516 + 512 * h], bank[:, :], ACT.Identity, bias=lnb, scale=lng),
                       t, S["xnT"], l_v, c_z)
                PM.free(i, c)
                cp.append(c)
            LNM.free(il, *trs)
            zz, uu, pr = [], [], []
            for h in range(2):
                for eb in range(2):
                    i, bank, w = PM.take()
                    t = pe(lambda e, h=h, eb=eb, bank=bank: e.matmul(bank[:, :], Win[:, 256 + 128 * eb:384 + 128 * eb],
                                                                    xnT[:, 4 + 512 * h:516 + 512 * h], start=True, stop=True), cp, l_win, w)
                    c = ac(lambda e, h=h, eb=eb, bank=bank: e.activation(zs[:, eb, 512 * h:512 * h + 512], bank[:, :], ACT.Silu), t, S["zs"])
                    PM.free(i, c)
                    zz.append(c)
                    i, bank, w = PM.take()
                    for k in range(KC):
                        t = pe(lambda e, k=k, h=h, eb=eb, bank=bank: e.matmul(
                            bank[:, :], Wk[:, k, 128 * eb:128 * eb + 128], xnT[:, 1 + k + 512 * h:513 + k + 512 * h],
                            start=(k == 0), stop=(k == KC - 1)), c_wk, w)
                    c = ac(lambda e, h=h, eb=eb, bank=bank: e.activation(u2[:, eb, 512 * h:512 * h + 512], bank[:, :], ACT.Silu,
                                                                        bias=cvb[:, eb:eb + 1]), t, S["u2"])
                    PM.free(i, c)
                    uu.append(c)
                    pr.append(t)
            S["xnT"] = pr
            bc, dtd, dud = [], [], []
            for h in range(2):
                hs = slice(512 * h, 512 * h + 512)
                i, bank, w = PM.take()
                for eb in range(2):
                    t = pe(lambda e, eb=eb, hs=hs, bank=bank: e.matmul(bank[0:104, :], Wx[:, eb, :], u2[:, eb, hs],
                                                                      start=(eb == 0), stop=(eb == 1)), uu, wx, w)
                jr, rb, wr = G.take()
                Rs = rb[:, 0, :]
                hm_ = rb[:, 1, :].bitcast(BF16)
                Hs, Ms = hm_[0:96, 0:512], hm_[0:96, 512:1024]
                c0 = ac(lambda e, bank=bank, Rs=Rs: e.copy(Rs[96:104, :], bank[96:104, :]), t, wr)
                c1 = ac(lambda e, bank=bank, Hs=Hs: e.copy(Hs, bank[0:96, :]), t, wr)
                c2 = dv(lambda e, bank=bank, Rs=Rs, Hs=Hs: e.tensor_tensor(Rs[0:96, :], bank[0:96, :], Hs, ALU.subtract), c1)
                PM.free(i, c0, c2)
                c3 = dv(lambda e, Rs=Rs, Ms=Ms: e.tensor_copy(Ms, Rs[0:96, :]), c2)
                c4 = dv(lambda e, hs=hs, Rs=Rs, Ms=Ms: e.tensor_tensor(BC[64:96, hs], Rs[64:96, :], Ms[64:96, :], ALU.subtract), c3, S["BC"])
                c5 = ac(lambda e, hs=hs, Hs=Hs: e.copy(BC[0:32, hs], Hs[0:32, :]), c1, S["BC"])
                c6 = ac(lambda e, hs=hs, Ms=Ms: e.copy(BC[32:64, hs], Ms[32:64, :]), c3, S["BC"])
                bc += [c4, c5, c6]
                for eb in range(2):
                    i, bank, w = PM.take()
                    t = pe(lambda e, eb=eb, bank=bank, Rs=Rs: e.matmul(bank[:, :], Wdt[96:104, 128 * eb:128 * eb + 128], Rs[96:104, :],
                                                               start=True, stop=True), c0, l_wdt, w)
                    bb = bdt[:, eb:eb + 1]
                    ja, pa, wpa = dA.take()
                    jb, pb, wpb = G.take()
                    s0_, s1_, s2_, s3_ = pa[:, 0:1, :], pa[:, 1:2, :], pb[:, 0:1, :], pb[:, 1:2, :]
                    s0_, s1_, s2_, s3_ = (v.rearrange("p a n -> p (a n)") for v in (s0_, s1_, s2_, s3_))
                    d1 = ac(lambda e, s0_=s0_, s1_=s1_, s2_=s2_, s3_=s3_, bank=bank, bb=bb: e.activation(s0_, bank[:, :], ACT.Relu, bias=bb), t, wpa)
                    d2 = ac(lambda e, s0_=s0_, s1_=s1_, s2_=s2_, s3_=s3_, bank=bank, bb=bb: e.activation(s1_, bank[:, :], ACT.Abs, bias=bb), t, wpa)
                    PM.free(i, d1, d2)
                    d3 = ac(lambda e, s0_=s0_, s1_=s1_, s2_=s2_, s3_=s3_: e.activation(s1_, s1_, ACT.Exp, scale=-1.0), d2)
                    d4 = dv(lambda e, s0_=s0_, s1_=s1_, s2_=s2_, s3_=s3_: e.tensor_scalar(s2_, s1_, 1.0, -1.0, ALU.add, ALU.add), d3, wpb)
                    d5 = ac(lambda e, s0_=s0_, s1_=s1_, s2_=s2_, s3_=s3_: e.activation(s3_, s1_, ACT.Ln, bias=1.0), d3, wpb)
                    d6 = po(lambda e, s0_=s0_, s1_=s1_, s2_=s2_, s3_=s3_: e.tensor_tensor(s2_, s1_, s2_, ALU.subtract), d4)
                    d7 = po(lambda e, s0_=s0_, s1_=s1_, s2_=s2_, s3_=s3_: e.tensor_tensor(s3_, s3_, s2_, ALU.add), d5, d6)
                    d8 = po(lambda e, s0_=s0_, s1_=s1_, s2_=s2_, s3_=s3_, eb=eb, hs=hs: e.tensor_tensor(dtb[:, eb, hs], s3_, s0_, ALU.add), d7, d1, S["dt"])
                    d9 = po(lambda e, s0_=s0_, s1_=s1_, s2_=s2_, s3_=s3_, eb=eb, hs=hs: e.tensor_tensor(dtu[:, eb, hs], dtb[:, eb, hs], u2[:, eb, hs], ALU.mult), d8, uu)
                    dA.free(ja, d8)
                    G.free(jb, d8)
                    dtd.append(d8)
                    dud.append(d9)
                G.free(jr, t, c4, c5, c6)
            xs, alls = [], []
            for h in range(2):
                hs = slice(512 * h, 512 * h + 512)
                yt = [None, None]
                held = [PM.take() for _ in range(4)]
                Y = [held[0][1], held[1][1]]
                BB, CB = held[2][1], held[3][1]
                ylast, S["bb"], S["cb"] = [held[0][2], held[1][2]], held[2][2], held[3][2]
                for n in range(NS):
                    tb = pe(lambda e, n=n, hs=hs, BB=BB: e.matmul(BB[:, :], idm[:, n:n + 1].to_broadcast((96, 128)), BC[:, hs], start=True, stop=True), bc, c_sel, S["bb"])
                    ig, gb, wg = G.take()
                    v1 = dv(lambda e, gb=gb, hs=hs, BB=BB: e.tensor_tensor(gb[:, :, :], BB[:, :].unsqueeze(1).to_broadcast((128, 2, 512)),
                                                                   dtu[:, :, hs], ALU.mult), tb, dud, wg)
                    S["bb"] = [v1]
                    ia, da, wa = dA.take()
                    es = [ac(lambda e, eb=eb, n=n, da=da, hs=hs: e.activation(da[:, eb, :], dtb[:, eb, hs], ACT.Exp, scale=An[:, eb, n:n + 1]),
                             dtd, c_an, wa) for eb in range(2)]
                    sc = [dv(lambda e, eb=eb, n=n, da=da, gb=gb, h=h: e.tensor_tensor_scan(
                        gb[:, eb, :], da[:, eb, :], gb[:, eb, :], 0.0 if h == 0 else hl[:, eb, n:n + 1], ALU.mult, ALU.add),
                        es[eb], v1, S["hl"] if h else None) for eb in range(2)]
                    dA.free(ia, *sc)
                    v3 = None
                    if h == 0:
                        v3 = dv(lambda e, n=n, gb=gb: e.tensor_copy(hl[:, :, n:n + 1], gb[:, :, 511:512]), sc, S["hl"], c_z)
                        alls.append(v3)
                    tcb = pe(lambda e, n=n, hs=hs, CB=CB: e.matmul(CB[:, :], idm[:, 16 + n:17 + n].to_broadcast((96, 128)), BC[:, hs],
                                                            start=True, stop=True), bc, S["cb"])
                    v2 = dv(lambda e, gb=gb, CB=CB: e.tensor_tensor(gb[:, :, :], CB[:, :].unsqueeze(1).to_broadcast((128, 2, 512)),
                                                            gb[:, :, :], ALU.mult), tcb, sc, v3)
                    S["cb"] = [v2]
                    for eb in range(2):
                        yt[eb] = pe(lambda e, eb=eb, n=n, gb=gb, Y=Y: e.matmul(Y[eb][:, :], ident, gb[:, eb, :], start=(n == 0), stop=(n == NS - 1)),
                                    v2, ylast)
                    G.free(ig, yt[1])
                if h == 0:
                    S["hl"] = alls
                jy, yg, wy = G.take()
                ys = [dv(lambda e, eb=eb, hs=hs, yg=yg, Y=Y: e.scalar_tensor_tensor(yg[:, eb, :], u2[:, eb, hs], Dp[:, eb:eb + 1], Y[eb][:, :],
                                                                              ALU.mult, ALU.add), yt[1], wy, l_v) for eb in range(2)]
                for k, x in ((0, ys[0]), (1, ys[1]), (2, v1), (3, v2)):
                    PM.free(held[k][0], x)
                gt = po(lambda e, hs=hs, yg=yg: e.tensor_tensor(yg[:, :, :], yg[:, :, :], zs[:, :, hs], ALU.mult), ys, zz)
                i, bank, w = PM.take()
                for k in range(4):
                    for eb in range(2):
                        t = pe(lambda e, k=k, eb=eb, bank=bank, yg=yg: e.matmul(
                            bank[:, 128 * k:128 * k + 128], yg[:, eb, 128 * k:128 * k + 128],
                            Wout[:, eb, :], start=(eb == 0), stop=(eb == 1)), gt, l_wo, w)
                G.free(jy, t)
                xv = X[:, 8 * b + 4 * h:8 * b + 4 * h + 4, :].rearrange("p a c -> p (a c)")
                x1 = dv(lambda e, xv=xv, bank=bank, h=h: e.scalar_tensor_tensor(
                    xv, bank[:, :], res, xv, ALU.mult, ALU.add), t, xa, no, l_res)
                PM.free(i, x1)
                xs.append(x1)
            S["zs"] = [gt]
            S["u2"] = [gt] + ys
            S["dt"] = sc + [v1]
            S["BC"] = [tcb]
            S["hl"] = sc
            xready[b] = xs

        outs = []

        def store(b):
            q.stream("ffn")
            outs.append(dma(lambda e: e.dma_start(out[b].rearrange("(i p) c -> p i c", p=128), X[:, 8 * b:8 * b + 8, :]), xready[b]))

        attention(0)
        ffn(0)
        for b in range(NB):
            if b + 1 < NB:
                attention(b + 1)
                ffn(b + 1)
            mamba(b)
            ffn(b)
            store(b)
        q.merge()

        sems = {e: ctx.enter_context(nc.semaphore(f"s_{e}")) for e in Queue.ENGINES}
        count = [0]

        def new_sem():
            count[0] += 1
            return ctx.enter_context(nc.semaphore(f"s_dma{count[0]}"))

        q.number(sems, new_sem)
        block = ctx.enter_context(nc.Block())

        @block.sync
        def _(eng):
            q.write("sync", eng)
            for t in outs:
                eng.wait_ge(t.sem, 16)

        @block.tensor
        def _(eng):
            q.write("tensor", eng)

        @block.vector
        def _(eng):
            q.write("vector", eng)

        @block.scalar
        def _(eng):
            q.write("scalar", eng)

        @block.gpsimd
        def _(eng):
            q.write("gpsimd", eng)


STREAMS = ("mamba", "attention", "ffn")

_INS = {"x": "L0_attn_a_x", "Wq": "L0_attn_a_Wq", "Wk": "L0_attn_a_Wk", "Wv": "L0_attn_a_Wv", "Wo": "L0_attn_a_Wo",
        "ln_g": "L0_attn_b_ln_g", "ln_b": "L0_attn_b_ln_b", "W_in": "L0_attn_b_W_in", "conv_w": "L0_attn_b_conv_w",
        "conv_b": "L0_attn_b_conv_b", "W_xp": "L0_attn_b_W_xp", "W_dt": "L0_attn_b_W_dt", "b_dt": "L0_attn_b_b_dt",
        "A_log": "L0_attn_b_A_log", "D_param": "L0_attn_b_D_param", "W_out": "L0_attn_b_W_out", "res": "L0_attn_b_res_scale",
        "k0": "L0_ffn_k0", "k1": "L0_ffn_k1", "k2": "L0_ffn_k2", "s0": "L0_ffn_s0", "s1": "L0_ffn_s1", "s2": "L0_ffn_s2"}


def kernel(**inputs):
    import numpy as _np
    import concourse.bacc as _bacc
    from concourse import mybir as _mybir
    from concourse.bass_utils import run_bass_kernel_spmd as _run

    nc = _bacc.Bacc("TRN2", target_bir_lowering=False, num_devices=1)
    arrays, args = {}, {}
    for short, name in _INS.items():
        a = _np.ascontiguousarray(inputs[name])
        if short in ("s0", "s1", "s2", "res"):
            a = a.reshape(1, 1)
        arrays[f"in_{short}"] = a
        args[short] = nc.dram_tensor(f"in_{short}", a.shape, _mybir.dt.from_np(a.dtype), kind="ExternalInput").ap()
    c = constants()
    arrays["in_consts"] = c
    args["consts"] = nc.dram_tensor("in_consts", c.shape, _mybir.dt.from_np(c.dtype), kind="ExternalInput").ap()
    o = nc.dram_tensor("out_0", (NB, T, C), _mybir.dt.float32, kind="ExternalOutput").ap()
    hybrid_block(nc, args, o)
    r = _run(nc, [arrays], core_ids=[0])
    return r.results[0]["out_0"]
```

```python
from contextlib import ExitStack

import numpy as np

import concourse.bass as bass
from concourse import mybir

F32 = mybir.dt.float32
BF16 = mybir.dt.bfloat16
F16 = mybir.dt.float16
U8 = mybir.dt.uint8
ALU = mybir.AluOpType
ACT = mybir.ActivationFunctionType
AX = mybir.AxisListType

NPA, POOL, WIDE = 3, 2, 3
NB, T, C, NH, HD = 4, 1024, 128, 16, 8
E2, NS, KC, RK = 2, 16, 4, 8
EPS = 1e-5
NEG = -1e30
TABLES = "natural_log_exp_and_others"

CONST = {}
_at = 0
for _name, _n in (("ident", 128), ("e32", 32), ("hmask", 4), ("dmask", 32), ("qmask", 4), ("hsel", 128)):
    CONST[_name] = (_at, _n)
    _at += _n
NCONST = _at
NMASK = 3 * 512


def constants():
    out = np.zeros((128, NCONST + NMASK), np.float32)

    def put(name, a):
        at, n = CONST[name]
        out[: a.shape[0], at:at + n] = a.reshape(a.shape[0], n)

    p = np.arange(128)
    put("ident", np.eye(128, dtype=np.float32))
    q, k = np.arange(32)[:, None], np.arange(64)[None, :]
    win = np.where((k <= q + 32) & (k >= q + 1), 0.0, NEG)
    first = np.where((k <= q + 32) & (k >= q + 1) & (k >= 32), 0.0, NEG)
    r, c = np.arange(32)[:, None], np.arange(32)[None, :]
    stride = np.where((r // 16 == c // 16) & (c % 16 < r % 16), 0.0, NEG)
    head = np.concatenate([first, win] * 4, 1)
    rest = np.concatenate([win] * 8, 1)
    far = np.concatenate([stride] * 16, 1)
    out[:, NCONST:] = np.tile(np.concatenate([head, rest, far], 1), (4, 1))
    put("e32", (p[:, None] % 32 == np.arange(32)[None, :]).astype(np.float32))
    put("hmask", (p[:, None] // 32 == np.arange(4)[None, :]).astype(np.float32))
    put("dmask", (p[:, None] // 32 == np.arange(32)[None, :] // 8).astype(np.float32))
    put("qmask", ((p[:, None] // 8 % 4 == np.arange(4)[None, :]) * float(HD) ** -0.5).astype(np.float32))
    put("hsel", (np.arange(16)[:, None] == p[None, :] // 8).astype(np.float32))
    return out


class Tok:

    def __init__(self, eng):
        self.eng, self.used, self.sem, self.value = eng, False, None, 0


def size(ap):
    n = 1
    for d in ap.shape[1:]:
        n *= d
    return n


class Costs:

    def __init__(self, name):
        self.name = name

    def plain(self, out, *_, **k):
        per, base = {"vector": (1.04, 60), "scalar": (0.84, 90), "gpsimd": (1.0, 100)}[self.name]
        return base + per * size(out)

    tensor_copy = tensor_scalar = scalar_tensor_tensor = tensor_tensor_scan = copy = activation = memset = bn_aggr = plain

    def bn_stats(self, out, in_):
        return self.plain(in_)

    def tensor_reduce(self, out, in_, *_):
        return self.plain(in_)

    def reciprocal(self, out, in_):
        return 60 + 6.3 * size(out)

    def tensor_tensor(self, out, a, b, op):
        if self.name == "gpsimd":
            return 100 + (169 if op == ALU.pow else 2.25) * size(out)
        return self.plain(out)

    def matmul(self, out, lhsT, rhs, **k):
        wide, load = max(64, size(rhs)) / 2.4, size(lhsT) / 1.2
        return 2 * max(2 * wide, load) if rhs.dtype == F32 else max(wide, load)

    def transpose(self, out, in_, ident):
        return 110

    def dma_start(self, *_, **k):
        return 2000

    def preload_act_table_set(self, *_):
        return 1300


class Queue:

    ENGINES = ("tensor", "vector", "scalar", "gpsimd", "sync")
    AFTER = {"tensor": 200, "vector": 80, "scalar": 120, "gpsimd": 100, "sync": 0}

    def __init__(self):
        self.streams, self.now = {}, None
        self.ops = {e: [] for e in self.ENGINES}
        self.costs = {e: Costs(e) for e in self.ENGINES}

    def stream(self, name):
        self.now = self.streams.setdefault(name, {e: [] for e in self.ENGINES})

    def add(self, eng, fn, waits, dma=False):
        tok = Tok(eng)
        tok.dma = dma
        flat, stack = [], [waits]
        while stack:
            w = stack.pop()
            if isinstance(w, Tok):
                w.used = True
                flat.append(w)
            elif w is not None:
                stack.extend(w)
        self.now[eng].append((flat, fn, tok, fn(self.costs[eng])))
        return tok

    def merge(self):
        free = {e: 0.0 for e in self.ENGINES}
        done = {}
        at = {(s, e): 0 for s in self.streams for e in self.ENGINES}
        left = sum(len(x) for v in self.streams.values() for x in v.values())
        while left:
            ready = []
            for e in self.ENGINES:
                for rank, s in enumerate(self.streams):
                    ops = self.streams[s][e]
                    if at[s, e] >= len(ops):
                        continue
                    flat, _, tok, cost = ops[at[s, e]]
                    start = free[e]
                    for w in flat:
                        if w not in done:
                            break
                        start = max(start, done[w])
                    else:
                        ready.append((start, rank, s, e))
            start, _, s, e = min(ready)
            flat, fn, tok, cost = self.streams[s][e][at[s, e]]
            at[s, e] += 1
            free[e] = start + cost
            done[tok] = start + cost + self.AFTER[e]
            if e == "sync":
                free[e] = start + 60
            self.ops[e].append((flat, fn, tok))
            left -= 1

    def number(self, sem_of_engine, new_sem):
        for e, ops in self.ops.items():
            n = 0
            for _, _, tok in ops:
                if tok.dma:
                    tok.sem, tok.value = new_sem(), 16
                elif tok.used:
                    n += 1
                    tok.sem, tok.value = sem_of_engine[e], n

    def write(self, name, eng):
        seen = {}
        for waits, fn, tok in self.ops[name]:
            need = {}
            for w in waits:
                k = id(w.sem)
                if k not in need or need[k].value < w.value:
                    need[k] = w
            for k, w in need.items():
                if seen.get(k, 0) < w.value:
                    eng.wait_ge(w.sem, w.value)
                    seen[k] = w.value
            ins = fn(eng)
            if tok.dma:
                ins.then_inc(tok.sem, 16)
            elif tok.used:
                ins.then_inc(tok.sem, 1)


class Slot:

    def __init__(self, buf):
        self.buf, self.last, self.held = buf, [], False


class Slots:

    def __init__(self, bufs):
        self.slots, self.n = [b if isinstance(b, Slot) else Slot(b) for b in bufs], 0
        self.bufs = [s.buf for s in self.slots]

    def take(self):
        s = self.slots[self.n % len(self.slots)]
        self.n += 1
        assert not s.held
        w, s.last, s.held = s.last, [], True
        return s, s.buf, w

    def free(self, s, *toks):
        s.held = False
        s.last.extend(toks)


def hybrid_block(nc, ins, out):
    ctx = ExitStack()
    with ctx:
        def sb(name, shape, dt=F32):
            return ctx.enter_context(nc.sbuf_tensor(name, shape, dt))

        q = Queue()
        for name in STREAMS:
            q.stream(name)
        q.stream("weights")

        def pe(fn, *w):
            return q.add("tensor", fn, w)

        def dv(fn, *w):
            return q.add("vector", fn, w)

        def ac(fn, *w):
            return q.add("scalar", fn, w)

        def po(fn, *w):
            return q.add("gpsimd", fn, w)

        def dma(fn, *w):
            return q.add("sync", fn, w, dma=True)

        banks = [Slot(ctx.enter_context(nc.psum_tensor(f"ps{i}", [128, 512], F32))) for i in range(8)]
        PA, PF, PM = Slots(banks[0:NPA]), Slots(banks[NPA:5]), Slots(banks[5:8])

        cst = sb("cst", [128, NCONST])

        def const(name, rows=128):
            at, n = CONST[name]
            return cst[0:rows, at:at + n]

        ident = const("ident")
        hmask = const("hmask")
        dmask = const("dmask")
        e32 = const("e32")
        masks = sb("masks", [128, 3, 512], BF16)
        e4 = sb("e4", [128, 128], BF16)
        idm = sb("idm", [96, 32], BF16)
        X = sb("X", [128, NB * 8, C])
        WT = sb("WT", [128, 4, 128])
        Win = sb("Win", [128, 256])
        Wk = sb("Wk", [128, KC, 256])
        Wxr = sb("Wxr", [128, 2, 40])
        Wx = sb("Wx", [128, 2, 104])
        Wdt = sb("Wdt", [128, 256])
        Wout = sb("Wout", [128, 2, 128])
        Al = sb("Al", [128, 2, NS])
        Ap = sb("Ap", [128, 2, NS])
        An = sb("An", [128, 2, NS])
        vec = sb("vec", [128, 16])
        bdt, cvb, Dp = vec[:, 0:2], vec[:, 2:4], vec[:, 4:6]
        lng, lnb, res = vec[:, 6:7], vec[:, 7:8], vec[:, 8:9]
        s3 = vec[:, 9:12]
        sgn = sb("sgn", [128, 8])
        fsc = sb("fsc", [128, 4])
        expo = sb("expo", [128, 8])
        w0 = sb("w0", [128, 512], F16)
        w1 = sb("w1", [128, 4, 512], F16)
        w2 = sb("w2", [128, 4, 128], F16)

        G = Slots([sb(f"g{i}", [128, 2, 512]) for i in range(4)])
        dA = Slots([sb(f"dA{i}", [128, 2, 512]) for i in range(2)])

        def flat(t):
            return t[:, :, :].rearrange("p a n -> p (a n)")

        mraw0, mraw1 = flat(G.bufs[0]), flat(G.bufs[1])
        cwr = flat(G.bufs[2])
        kraw = flat(G.bufs[3]).bitcast(U8)
        k0r = kraw[:, 0:1024].rearrange("p (a n) -> p a n", a=2)
        k1r = kraw[:, 1024:3072].rearrange("p (a n) -> p a n", a=4)
        k2r = kraw[:, 3072:3584].rearrange("p (a n) -> p a n", a=4)
        Wraw = flat(dA.bufs[0])[:, 0:512].rearrange("p (a n) -> p a n", a=4)
        kt = flat(dA.bufs[1])[:, 0:512]

        def load(dst, src):
            def go(e):
                with nc.allow_non_contiguous_dma(reason="small vectors"):
                    return e.dma_start(dst, src)
            return dma(go)

        l_x = [None] * NB

        def load_x(b):
            l_x[b] = load(X[:, 8 * b:8 * b + 8, :], ins["x"][b].rearrange("(i p) c -> p i c", p=128))

        load_x(0)
        l_cst = load(cst[:, :], ins["consts"][:, 0:NCONST])
        l_m = [load(mraw0, ins["consts"][:, NCONST:NCONST + 1024]), load(mraw1[:, 0:512], ins["consts"][:, NCONST + 1024:])]
        l_w = [load(Wraw[:, i, :], ins[n]) for i, n in enumerate(("Wq", "Wk", "Wv", "Wo"))]
        l_s = [load(vec[:, 9 + i:10 + i], ins[f"s{i}"].to_broadcast((128, 1))) for i in range(3)]
        l_k0 = load(k0r, ins["k0"].rearrange("(a p) n -> p a n", p=128))
        l_k1 = load(k1r, ins["k1"].rearrange("(a p) n -> p a n", p=128))
        l_k2 = load(k2r, ins["k2"].rearrange("(a p) n -> p a n", p=128))
        l_wu = load(mraw1[:, 512:768], ins["W_in"][:, 0:256])
        l_win = load(Win[:, :], ins["W_in"][:, 256:512])
        l_cw = load(cwr, ins["conv_w"].rearrange("(o e) k -> o (e k)", o=1).to_broadcast((128, 256 * KC)))
        l_wx = load(Wxr[:, :, :], ins["W_xp"].rearrange("(a p) n -> p a n", p=128))
        l_wdt = load(Wdt[96:104, :], ins["W_dt"])
        l_wo = load(Wout[:, :, :], ins["W_out"].rearrange("(a p) n -> p a n", p=128))
        l_al = load(Al[:, :, :], ins["A_log"].rearrange("(a p) n -> p a n", p=128))
        l_v = [load(vec[:, 2 * i:2 * i + 2], ins[n].rearrange("(a p) -> p a", p=128))
               for i, n in enumerate(("b_dt", "conv_b", "D_param"))]
        l_v += [load(vec[:, 6 + i:7 + i], ins[n].rearrange("(p o) -> p o", o=1)) for i, n in enumerate(("ln_g", "ln_b"))]
        l_res = load(vec[:, 8:9], ins["res"].to_broadcast((128, 1)))
        for b in range(1, NB):
            load_x(b)

        mk_ = masks[:, :, :].rearrange("p a n -> p (a n)")
        c_mask = [dv(lambda e: e.tensor_copy(mk_[:, 0:1024], mraw0), l_m[0]), dv(lambda e: e.tensor_copy(mk_[:, 1024:1536], mraw1[:, 0:512]), l_m[1])]
        c_e4 = [dv(lambda e, k=k: e.tensor_copy(e4[:, 32 * k:32 * k + 32], ident[:, 0:32]), l_cst) for k in range(4)]
        c_sel = dv(lambda e: e.tensor_copy(idm[:, :], e32[0:96, :]), l_cst)
        c_expo = po(lambda e: e.memset(expo[:, :], -0.5))
        i, bank, w = PA.take()
        for j in range(4):
            t_w = pe(lambda e, j=j, bank=bank: e.transpose(bank[:, 128 * j:128 * j + 128], Wraw[:, j, :], ident), l_w[j], l_cst, w)
        c_wt = ac(lambda e, bank=bank: e.copy(WT[:, :, :].rearrange("p a n -> p (a n)"), bank[:, :]), t_w)
        PA.free(i, c_wt)
        dA.free(dA.slots[0], t_w)

        g1 = dv(lambda e: e.tensor_scalar(sgn[:, 0:3], s3, 0.0, None, ALU.is_gt), l_s)
        g2 = dv(lambda e: e.tensor_scalar(sgn[:, 3:6], s3, 0.0, None, ALU.is_lt), l_s)
        g3 = dv(lambda e: e.tensor_tensor(sgn[:, 0:3], sgn[:, 0:3], sgn[:, 3:6], ALU.subtract), g1, g2)
        g4 = dv(lambda e: e.tensor_tensor(fsc[:, 0:3], sgn[:, 0:3], s3, ALU.mult), g3)
        g5 = dv(lambda e: e.tensor_tensor(fsc[:, 3:4], fsc[:, 0:1], fsc[:, 1:2], ALU.mult), g4)
        c_f = dv(lambda e: e.tensor_scalar(fsc[:, 3:4], fsc[:, 3:4], s3[:, 2:3], 64.0, ALU.mult, ALU.mult), g5)
        FS = fsc[:, 3:4]
        g6 = dv(lambda e: e.tensor_scalar(sgn[:, 3:5], sgn[:, 0:2], 2.0, None, ALU.mult), g3)
        g7 = dv(lambda e: e.tensor_scalar(sgn[:, 4:5], sgn[:, 1:2], 0.125, None, ALU.mult), g6)
        g8 = dv(lambda e: e.tensor_tensor(kt, k0r[:, 0, :], k0r[:, 1, :], ALU.subtract), l_k0)
        c_w0 = dv(lambda e: e.tensor_scalar(w0[:, :], kt, sgn[:, 3:4], None, ALU.mult), g8, g6)
        c_w1 = dv(lambda e: e.tensor_scalar(w1[:, :, :].rearrange("p a n -> p (a n)"), kraw[:, 1024:3072],
                                            0.5, sgn[:, 4:5], ALU.subtract, ALU.mult), g7, l_k1)
        c_w2 = dv(lambda e: e.tensor_scalar(w2[:, :, :].rearrange("p a n -> p (a n)"), kraw[:, 3072:3584],
                                            2.0, 1.0, ALU.mult, ALU.subtract), l_k2)

        cwv = cwr.rearrange("p (e k) -> p k e", k=KC)
        c_wk = dv(lambda e: e.tensor_tensor(Wk[:, :, :], cwv, mraw1[:, 512:768].unsqueeze(1).to_broadcast((128, KC, 256)), ALU.mult),
                  l_wu, l_cw)
        G.free(G.slots[0], c_mask)
        G.free(G.slots[1], c_mask, c_wk)
        G.free(G.slots[2], c_wk)
        G.free(G.slots[3], c_w0, c_w1, c_w2)
        dA.free(dA.slots[1], c_w0)
        wx = [dv(lambda e, r=r: e.tensor_copy(Wx[:, :, 32 * r:32 * r + 32], Wxr[:, :, 8:40]), l_wx) for r in range(3)]
        wx.append(dv(lambda e: e.tensor_copy(Wx[:, :, 96:104], Wxr[:, :, 0:8]), l_wx))
        ac(lambda e: e.preload_act_table_set(TABLES))
        a1 = ac(lambda e: e.activation(Ap[:, :, :], Al[:, :, :], ACT.Exp), l_al)
        c_an = dv(lambda e: e.tensor_scalar(An[:, :, :], Ap[:, :, :], -1.0, None, ALU.mult), a1)

        xready = [[l_x[b]] * 8 for b in range(NB)]

        small = {n: [Slots([sb(f"{n}{k}", [128] + d)]) for k, d in (("st", [8, 6]), ("mv", [8, 2]), ("rs", [2, 8]))]
                 for n in STAGES}
        LNA = Slots([sb("lna", [128, 8, C])])
        aP = flat(LNA.bufs[0])
        LNF = Slots([sb("lnf", [128, 4, C])])

        aT = sb("aT", [128, 32 + T])
        KD = sb("KD", [128, 4, 32 + T])
        QT = sb("QT", [128, T])
        QM = Slots([sb(f"qm{i}", [128, 8, 4, 32]) for i in range(2)])
        V1 = Slots([sb(f"v1{i}", [128, 4, 2, 4, 33]) for i in range(2)])
        V2 = Slots([sb(f"v2{i}", [128, 2, 4, 4, 33]) for i in range(2)])
        Sx = Slots([sb(f"sx{i}", [128, 512]) for i in range(2)])
        PT = Slots([sb(f"pt{i}", [128, 4, 128]) for i in range(2)])
        mx = Slots([sb(f"mx{i}", [128, 16]) for i in range(4)])
        OM = Slots([sb(f"om{i}", [128, 4, 4, 32]) for i in range(2)])
        LM = Slots([sb(f"lm{i}", [128, 2, 4, 4, 4]) for i in range(2)])
        far = sb("far", [128, T])
        farc = sb("farc", [16, 2, T])
        near = Slots([sb(f"near{i}", [128, 256]) for i in range(1)])
        nearc = Slots([sb(f"nearc{i}", [16, 2, 256]) for i in range(1)])
        tmp = sb("tmp", [128, 2, 256])
        tmc = aP[0:16, :].rearrange("p (a n) -> p a n", a=4)

        H0 = Slots([sb(f"h0{i}", [128, 2, 4, 512], F16) for i in range(1)])
        H1 = Slots([sb(f"h1{i}", [128, 2, 4, 512], F16) for i in range(1)])
        BS = Slots([sb(f"bs{i}", [128, 512]) for i in range(3)])

        xnT = sb("xnT", [128, 4 + T])
        zs = sb("zs", [128, 2, T])
        u2 = sb("u2", [128, 2, T])
        dtb = sb("dtb", [128, 2, T])
        dtu = sb("dtu", [128, 2, T])
        BC = sb("BC", [96, T], BF16)
        hl = sb("hl", [128, 2, NS])

        z = [po(lambda e: e.memset(aT[:, 0:32], 0.0)), po(lambda e: e.memset(KD[:, :, :], 0.0)),
             po(lambda e: e.memset(xnT[:, 0:4], 0.0)), po(lambda e: e.memset(hl[:, :, :], 0.0))]
        ones = []
        for v, n in ((V1.bufs[0], 2), (V1.bufs[1], 2), (V2.bufs[0], 4), (V2.bufs[1], 4)):
            zv = po(lambda e, v=v: e.memset(v[:, :, :, :, :], 0.0))
            r = 128 // n
            ones += [dv(lambda e, k=k, v=v, r=r: e.memset(v[r * k:r * k + r, :, k, :, 32], 1.0), zv) for k in range(n)]
        c_z = z + ones

        def norm(name, src, ks, ready, dst, dwait):
            n = len(ks)
            st, mv, rs = small[name]
            i1, s_, w1_ = st.take()
            i2, m_, w2_ = mv.take()
            i3, r_, w3_ = rs.take()
            ag = []
            ss = [dv(lambda e, j=j, k=k: e.bn_stats(s_[:, j, :], src(k)), ready[k], w1_) for j, k in enumerate(ks)]
            for j in range(n):
                ag.append(dv(lambda e, j=j: e.bn_aggr(m_[:, j, :], s_[:, j, :]), ss[j], w2_))
            st.free(i1, *ag)
            a = po(lambda e: e.tensor_scalar(r_[:, 1, 0:n], m_[:, 0:n, 1], 1.0, EPS, ALU.mult, ALU.add), ag, w3_)
            p = po(lambda e: e.tensor_tensor(r_[:, 0, 0:n], r_[:, 1, 0:n], expo[:, 0:n], ALU.pow), a, c_expo)
            m1 = po(lambda e: e.tensor_tensor(r_[:, 1, 0:n], m_[:, 0:n, 0], r_[:, 0, 0:n], ALU.mult), p)
            m2 = po(lambda e: e.tensor_scalar(r_[:, 1, 0:n], r_[:, 1, 0:n], -1.0, 0.0, ALU.mult, ALU.add), m1)
            mv.free(i2, m1)
            o = [po(lambda e, j=j, k=k: e.tensor_scalar(dst(k), src(k), r_[:, 0, j:j + 1], r_[:, 1, j:j + 1], ALU.mult, ALU.add),
                    m2, ready[k], dwait) for j, k in enumerate(ks)]
            rs.free(i3, *o)
            return dict(zip(ks, o))

        state = {n: [] for n in ("attn_in", "olm", "qk", "tmp", "xnT", "zs", "u2", "dt", "BC", "hl")}

        def attention(b):
            q.stream("attention")
            S = state
            il, A, wl = LNA.take()
            no = norm("attention", lambda k: X[:, 8 * b + k, :], range(8), xready[b], lambda k: A[:, k, :], wl)
            tr, cp = [], []
            for h in range(2):
                i, bank, w = PA.take()
                for k in range(4):
                    t = pe(lambda e, k=k, h=h, bank=bank: e.transpose(bank[:, 128 * k:128 * k + 128], A[:, 4 * h + k, :], ident),
                           no[4 * h + k], w, l_cst)
                    tr.append(t)
                c = ac(lambda e, h=h, bank=bank: e.copy(aT[:, 32 + 512 * h:32 + 512 * h + 512], bank[:, :]), t, S["attn_in"], c_z)
                cp.append(c)
                PA.free(i, c)
            aPd = [po(lambda e, g=g: e.tensor_scalar(
                aP[:, 512 * g:512 * g + 512].rearrange("p (r j) -> p r j", j=16),
                aT[:, 32:32 + T].rearrange("p (j r) -> p r j", r=64)[:, 32 * g:32 * g + 32, :], 1.0, 0.0, ALU.mult, ALU.add),
                cp, tr) for g in range(2)]
            qk_done, q_done, k_done = [], [], []
            for h in range(2):
                i, bank, w = PA.take()
                t = pe(lambda e, h=h, bank=bank: e.matmul(bank[:, :], WT[:, 0, :], aT[:, 32 + 512 * h:544 + 512 * h], start=True, stop=True),
                       c_wt, cp, w)
                qk_done.append(t)
                c = ac(lambda e, h=h, bank=bank: e.copy(QT[:, 512 * h:512 * h + 512], bank[:, :]), t, S["qk"])
                q_done.append(c)
                PA.free(i, c)
                i, bank, w = PA.take()
                t = pe(lambda e, h=h, bank=bank: e.matmul(bank[:, :], WT[:, 1, :], aT[:, 32 + 512 * h:544 + 512 * h], start=True, stop=True), w)
                qk_done.append(t)
                cs = [ac(lambda e, h=h, a=a, bank=bank: e.copy(KD[32 * a:32 * a + 32, a, 32 + 512 * h:544 + 512 * h], bank[32 * a:32 * a + 32, :]),
                         t, S["qk"], c_z) for a in range(4)]
                k_done += cs
                PA.free(i, *cs)
            aw = aT[:, :]

            def values(kind, g, cp=cp):
                i, bank, w = PA.take()
                iv, V, wv = (V1, V2)[kind].take()
                nk = (4, 2)[kind]
                for k in range(nk):
                    m = nk * g + k
                    if kind:
                        t = pe(lambda e, k=k, m=m, bank=bank: e.matmul(
                            bank[:, 128 * k:128 * k + 128], aP[:, 128 * m:128 * m + 128], WT[:, 2, :], start=True, stop=True), aPd, w)
                        continue
                    for s in range(2):
                        t = pe(lambda e, k=k, m=m, s=s, bank=bank: e.matmul(
                            bank[64 * s:64 * s + 64, 128 * k:128 * k + 128],
                            aw[:, 64 * m + 32 * s:64 * m + 32 * s + 64], WT[:, 2, :], start=True, stop=True), cp, w)
                qk_done.append(t)
                r = (64, 32)[kind]
                vs = [ac(lambda e, s=s: e.copy(V[r * s:r * s + r, :, s, :, 0:32],
                                               bank[r * s:r * s + r, 0:128 * nk].rearrange("p (k a d) -> p k a d", k=nk, a=4)), t, wv, c_z)
                      for s in range(128 // r)]
                PA.free(i, *vs)
                return iv, V, vs

            Qs = QT[:, :].rearrange("p (j r) -> p r j", r=64)
            qmask = const("qmask")
            Ks = KD[:, :, 32:32 + T].rearrange("p a (j r) -> p a r j", r=64)
            s_last, farm, merged, atts, q_read = [], [], [], [], []

            def prepare(kind, g):
                q.stream("prepare")
                iv, V, v_done = values(kind, g)
                iq, qt, wq = QM.take()
                at, done = 8 * g, []
                for j in range(4):
                    if kind:
                        src = Qs[:, 2 * at:2 * at + 16, :].rearrange("p (a r) j -> p a r j", r=2)
                        dst = qt[:, :, j, :].rearrange("p a (r j) -> p a r j", r=2)
                    else:
                        src = QT[:, 32 * at:32 * at + 256].rearrange("p (a n) -> p a n", n=32)
                        dst = qt[:, :, j, :]
                    done.append(po(lambda e, src=src, dst=dst, j=j: e.tensor_scalar(dst, src, qmask[:, j:j + 1], 0.0, ALU.mult, ALU.add),
                                   q_done, wq, l_cst))
                q_read.extend(done)
                return iv, V, v_done, iq, qt, done

            groups = [(kind, g) for kind in (1, 0) for g in range(4)]
            ready = prepare(*groups[0])
            for gi, (kind, g) in enumerate(groups):
                kw, nw, per = ((64, 2, 2), (32, 4, 1))[kind]
                nq = 8
                iv, V, v_done, iq, qm, qm_done = ready
                if kind == 0:
                    inr, nr, wn = near.take()
                    inc, nc_, wnc = nearc.take()
                    olm = []
                tails, reads = [], []
                for u in range(2):
                    io, om, wo_ = OM.take()
                    im, lm, wm_ = LM.take()
                    packed = []
                    for kk in range(per * u, per * u + per):
                        q.stream(f"heads{kk % WIDE}")
                        i, bank, w = PA.take()
                        mk = 2 if kind else (0 if g == kk == 0 else 1)
                        pe(lambda e, mk=mk, bank=bank: e.matmul(bank[:, :], e4[:, :], masks[:, mk, :], start=True,
                                                               stop=False, skip_group_check=True), c_mask, c_e4, w)
                        bw = bank[:, :].rearrange("p (a w k) -> p a w k", a=4, w=nw)
                        for k in range(nw):
                            wi = nw * kk + k
                            m = nq * g + wi
                            lq = qm[:, wi, :, :].rearrange("p a n -> p (a n)")
                            if kind == 0:
                                rk, dst = KD[:, :, 32 * m:32 * m + 64], bw[:, :, k, :]
                            else:
                                rk, dst = Ks[:, :, 2 * m:2 * m + 2, :], bw[:, :, k, :].rearrange("p a (r j) -> p a r j", r=2)
                            t = pe(lambda e, lq=lq, rk=rk, dst=dst, k=k, nw=nw: e.matmul(
                                dst, lq, rk, start=False, stop=(k == nw - 1), skip_group_check=True), qm_done, k_done)
                        s_last.append(t)
                        reads.append(t)
                        na = 4 * nw
                        ix, mm, wx_ = mx.take()
                        sv = bank[:, :].rearrange("p (a k) -> p a k", k=kw)
                        t = dv(lambda e, mm=mm, sv=sv, na=na: e.tensor_reduce(mm[:, 0:na], sv, AX.X, ALU.max), t, wx_)
                        isx, sx, ws_ = Sx.take()
                        t2 = dv(lambda e, mm=mm, sv=sv, sx=sx, na=na, kw=kw: e.tensor_tensor(
                            sx[:, :].rearrange("p (a k) -> p a k", k=kw), sv, mm[:, 0:na].unsqueeze(2).to_broadcast((128, na, kw)),
                            ALU.subtract), t, ws_)
                        PA.free(i, t2)
                        t3 = ac(lambda e, sx=sx: e.activation(sx[:, :], sx[:, :], ACT.Exp), t2)
                        w0_ = nw * (kk - per * u)
                        pk = dv(lambda e, mm=mm, lm=lm, na=na, nw=nw, w0_=w0_: e.tensor_tensor(
                            lm[:, 1, w0_:w0_ + nw, :, :], mm[:, 0:na].rearrange("p (a w) -> p w a", w=nw).unsqueeze(3).to_broadcast((128, nw, 4, 4)),
                            hmask.unsqueeze(1).unsqueeze(1).to_broadcast((128, nw, 4, 4)), ALU.mult), t, wm_)
                        mx.free(ix, pk, t2)
                        packed.append(pk)
                        i, bank, w = PA.take()
                        for k in range(4):
                            t4 = pe(lambda e, k=k, bank=bank, sx=sx: e.transpose(bank[:, 128 * k:128 * k + 128], sx[:, 128 * k:128 * k + 128], ident),
                                    t3, w)
                        Sx.free(isx, t4)
                        ip, pt, wp_ = PT.take()
                        t5 = ac(lambda e, pt=pt, bank=bank: e.copy(pt[:, :, :].rearrange("p a n -> p (a n)"), bank[:, :]), t4, wp_)
                        PA.free(i, t5)
                        ng = 8 // nw
                        for o in range(4 // ng):
                            i, bank, w = PA.take()
                            bo = bank[:, 0:264].rearrange("p (w a n) -> p w a n", w=nw, a=ng)
                            for k in range(ng):
                                a = ng * o + k
                                t6 = pe(lambda e, k=k, a=a, bo=bo, pt=pt, V=V, kk=kk: e.matmul(
                                    bo[:, :, k, :], pt[:, a, :], V[:, kk, :, a, :], start=True, stop=True), t5, v_done, w)
                            ws, gs = slice(w0_, w0_ + nw), slice(ng * o, ng * o + ng)
                            t7 = dv(lambda e, bo=bo, om=om, ws=ws, gs=gs, nw=nw, ng=ng: e.tensor_tensor(
                                om[:, ws, gs, :], bo[:, :, :, 0:32], dmask.unsqueeze(1).unsqueeze(1).to_broadcast((128, nw, ng, 32)),
                                ALU.mult), t6, wo_)
                            t8 = dv(lambda e, bo=bo, lm=lm, ws=ws, gs=gs, nw=nw, ng=ng: e.tensor_tensor(
                                lm[:, 0, ws, gs, :], bo[:, :, :, 32:33].to_broadcast((128, nw, ng, 4)),
                                hmask.unsqueeze(1).unsqueeze(1).to_broadcast((128, nw, ng, 4)), ALU.mult), t6, wm_)
                            PA.free(i, t7, t8)
                            packed += [t7, t8]
                        PT.free(ip, t6)
                        tails.append(t6)
                    if u == 0 and gi + 1 < len(groups):
                        ready = prepare(*groups[gi + 1])
                        q.stream(f"heads{kk % WIDE}")
                    i, bank, w = PA.take()
                    for k in range(4):
                        t1 = pe(lambda e, k=k, om=om, bank=bank: e.matmul(
                            bank[:, 32 * k:32 * k + 32], om[:, k, :, :].rearrange("p a n -> p (a n)"), e32, start=True, stop=True), packed, w)
                    for x in range(2):
                        for k in range(4):
                            t2 = pe(lambda e, k=k, x=x, lm=lm, bank=bank: e.matmul(
                                bank[0:16, 128 + 128 * x + 32 * k:160 + 128 * x + 32 * k], lm[:, x, k, :, :].rearrange("p a b -> p (a b)"),
                                e32, start=True, stop=True))
                    OM.free(io, t1)
                    LM.free(im, t2)
                    if kind == 0:
                        c1 = ac(lambda e, nr=nr, bank=bank, u=u: e.copy(nr[:, 128 * u:128 * u + 128], bank[:, 0:128]), t2, wn)
                        c2 = ac(lambda e, nc_=nc_, bank=bank, u=u: e.copy(nc_[:, :, 128 * u:128 * u + 128],
                                                                         bank[0:16, 128:384].rearrange("p (a n) -> p a n", a=2)), t2, wnc)
                        olm += [c1, c2]
                        PA.free(i, c1, c2)
                    else:
                        at = 2 * (nq * g + 4 * u)
                        dst = far[:, :].rearrange("p (j r) -> p r j", r=64)[:, at:at + 8, :]
                        v1 = bank[:, 0:128].rearrange("p (r j) -> p r j", j=16)
                        c1 = ac(lambda e, dst=dst, v1=v1: e.copy(dst, v1), t2, S["olm"])
                        dsc = farc[:, :, :].rearrange("p a (j r) -> p a r j", r=64)[:, :, at:at + 8, :]
                        v2 = bank[0:16, 128:384].rearrange("p (a r j) -> p a r j", a=2, j=16)
                        c2 = ac(lambda e, dsc=dsc, v2=v2: e.copy(dsc, v2), t2, S["olm"])
                        farm += [c1, c2]
                        PA.free(i, c1, c2)
                (V1, V2)[kind].free(iv, *tails)
                QM.free(iq, *reads)
                q.stream("join")
                if kind:
                    continue
                cols = slice(256 * g, 256 * g + 256)
                L1, M1 = nc_[:, 0, :], nc_[:, 1, :]
                L2, M2 = farc[:, 0, cols], farc[:, 1, cols]
                ta = dv(lambda e, M1=M1, M2=M2: e.tensor_tensor(tmc[:, 2, :], M1, M2, ALU.max), olm, farm, S["tmp"], qk_done)
                tb = po(lambda e, M1=M1: e.tensor_tensor(tmc[:, 0, :], M1, tmc[:, 2, :], ALU.subtract), ta)
                tc_ = po(lambda e, M2=M2: e.tensor_tensor(tmc[:, 1, :], M2, tmc[:, 2, :], ALU.subtract), ta)
                td = ac(lambda e: e.activation(tmc[:, 0:2, :], tmc[:, 0:2, :], ACT.Exp), tb, tc_)
                f1 = po(lambda e, L1=L1: e.tensor_tensor(tmc[:, 2, :], L1, tmc[:, 0, :], ALU.mult), td)
                f2 = po(lambda e, L2=L2: e.tensor_tensor(tmc[:, 3, :], L2, tmc[:, 1, :], ALU.mult), td)
                f3 = po(lambda e: e.tensor_tensor(tmc[:, 2, :], tmc[:, 2, :], tmc[:, 3, :], ALU.add), f1, f2)
                f4 = dv(lambda e: e.reciprocal(tmc[:, 2, :], tmc[:, 2, :]), f3)
                f5 = po(lambda e: e.tensor_tensor(tmc[:, 0, :], tmc[:, 0, :], tmc[:, 2, :], ALU.mult), f4)
                f6 = po(lambda e: e.tensor_tensor(tmc[:, 1, :], tmc[:, 1, :], tmc[:, 2, :], ALU.mult), f4)
                nearc.free(inc, f1, ta, tb)
                i, bank, w = PA.take()
                f7 = pe(lambda e, bank=bank: e.matmul(bank[:, :], const("hsel", 16), tmc[:, 0:2, :], start=True, stop=True), f5, f6, w)
                O2 = far[:, cols]
                ATT = tmp[:, 0, :]
                h1 = dv(lambda e, bank=bank, nr=nr: e.tensor_tensor(tmp[:, 0, :], bank[:, 0:256], nr[:, :], ALU.mult), f7)
                h2 = dv(lambda e, bank=bank, O2=O2: e.tensor_tensor(tmp[:, 1, :], bank[:, 256:512], O2, ALU.mult), f7)
                PA.free(i, h1, h2)
                f8 = dv(lambda e: e.tensor_tensor(tmp[:, 0, :], tmp[:, 0, :], tmp[:, 1, :], ALU.add), h1, h2)
                near.free(inr, h1)
                merged += [h2, f2, ta, tc_]
                i, bank, w = PA.take()
                for k in range(2):
                    t = pe(lambda e, k=k, bank=bank: e.matmul(bank[:, 128 * k:128 * k + 128], ATT[:, 128 * k:128 * k + 128], WT[:, 3, :],
                                                             start=True, stop=True), f8, w)
                xv = X[:, 8 * b + 2 * g:8 * b + 2 * g + 2, :].rearrange("p a c -> p (a c)")
                x1 = dv(lambda e, xv=xv, bank=bank: e.tensor_tensor(xv, bank[:, 0:256], xv, ALU.add), t, [no[2 * g], no[2 * g + 1]])
                PA.free(i, x1)
                atts.append(x1)
                S["tmp"] = [t, f7]
                merged += [f7, h2, f3]
            S["attn_in"] = qk_done + aPd
            LNA.free(il, *(qk_done + S["tmp"] + merged))
            S["qk"] = s_last + q_read
            S["olm"] = merged
            xready[b] = [atts[k // 2] for k in range(8)]

        def ffn(b):
            q.stream("ffn")
            xs = []
            for h in range(2):
                il, A, wl = LNF.take()
                no = norm("ffn", lambda k: X[:, 8 * b + k, :], range(4 * h, 4 * h + 4), xready[b], lambda k, h=h, A=A: A[:, k - 4 * h, :], wl)
                i, bank, w = PF.take()
                for k in range(4):
                    t = pe(lambda e, k=k, A=A, bank=bank: e.transpose(bank[:, 128 * k:128 * k + 128], A[:, k, :], ident),
                           no[4 * h + k], w, l_cst)
                LNF.free(il, t)
                i1, h1, wh1 = H1.take()
                fa = h1[:, 0, 0:2, :]
                c1 = ac(lambda e, fa=fa, bank=bank: e.copy(fa[:, 0, :], bank[:, :]), t, wh1)
                c2 = dv(lambda e, fa=fa, bank=bank: e.tensor_tensor(fa[:, 1, :], bank[:, :], fa[:, 0, :], ALU.subtract), c1, wh1)
                PF.free(i, c2)
                ih, h0, wh = H0.take()
                r0 = []
                for mo in range(4):
                    i, bank, w = PF.take()
                    for s in range(2):
                        t = pe(lambda e, s=s, mo=mo, fa=fa, bank=bank: e.matmul(bank[:, :], w0[:, 128 * mo:128 * mo + 128], fa[:, s, :],
                                                                               start=(s == 0), stop=(s == 1)), c1, c2, c_w0, w)
                    e1 = ac(lambda e, mo=mo, h0=h0, bank=bank: e.activation(h0[:, 0, mo, :], bank[:, :], ACT.Relu), t, wh)
                    e2 = dv(lambda e, mo=mo, h0=h0, bank=bank: e.scalar_tensor_tensor(h0[:, 1, mo, :], bank[:, :], 0.0, h0[:, 0, mo, :],
                                                                                    ALU.max, ALU.subtract), e1, wh)
                    PF.free(i, e2)
                    r0.append(e2)
                fr = t
                r1 = []
                for mo in range(4):
                    i, bank, w = PF.take()
                    n = 0
                    for ki in range(4):
                        for s in range(2):
                            t = pe(lambda e, s=s, mo=mo, ki=ki, n=n, h0=h0, bank=bank: e.matmul(
                                bank[:, :], w1[:, ki, 128 * mo:128 * mo + 128], h0[:, s, ki, :], start=(n == 0), stop=(n == 7)), r0[ki], c_w1, w)
                            n += 1
                    e1 = ac(lambda e, mo=mo, h1=h1, bank=bank: e.activation(h1[:, 0, mo, :], bank[:, :], ACT.Relu), t, fr)
                    e2 = dv(lambda e, mo=mo, h1=h1, bank=bank: e.scalar_tensor_tensor(h1[:, 1, mo, :], bank[:, :], 0.0, h1[:, 0, mo, :],
                                                                                    ALU.max, ALU.subtract), e1, fr)
                    PF.free(i, e2)
                    r1.append(e2)
                H0.free(ih, t)
                i, bank, w = PF.take()
                for k in range(4):
                    n = 0
                    for ki in range(4):
                        for s in range(2):
                            t = pe(lambda e, s=s, k=k, ki=ki, n=n, h1=h1, bank=bank: e.matmul(
                                bank[:, 128 * k:128 * k + 128], h1[:, s, ki, 128 * k:128 * k + 128], w2[:, ki, :],
                                start=(n == 0), stop=(n == 7)), r1[ki], c_w2, w)
                            n += 1
                H1.free(i1, t)
                xv = X[:, 8 * b + 4 * h:8 * b + 4 * h + 4, :].rearrange("p a c -> p (a c)")
                x1 = dv(lambda e, xv=xv, bank=bank: e.scalar_tensor_tensor(xv, bank[:, :], FS, xv, ALU.mult, ALU.add), t, *no.values(), c_f)
                PF.free(i, x1)
                xs.append(x1)
            xready[b] = [xs[k // 4] for k in range(8)]

        def mamba(b):
            q.stream("mamba")
            S = state
            il, A, wl = G.take()
            A = flat(A).rearrange("p (a n) -> p a n", a=8)
            trs, cp, xa, zz, pr = [], [], [], [], []
            for h in range(2):
                ks = range(4 * h, 4 * h + 4)
                no = norm("mamba", lambda k: X[:, 8 * b + k, :], ks, xready[b], lambda k: A[:, k, :], wl)
                xa.append(po(lambda e, h=h: e.tensor_tensor(X[:, 8 * b + 4 * h:8 * b + 4 * h + 4, :], X[:, 8 * b + 4 * h:8 * b + 4 * h + 4, :],
                                                            A[:, 4 * h:4 * h + 4, :], ALU.add), *no.values()))
                no2 = norm("mamba", lambda k: A[:, k, :], ks, no, lambda k: A[:, k, :], xa[h])
                i, bank, w = PM.take()
                for k in range(4):
                    t = pe(lambda e, k=k, h=h, bank=bank: e.transpose(bank[:, 128 * k:128 * k + 128], A[:, 4 * h + k, :], ident),
                           no2[4 * h + k], w)
                trs.append(t)
                c = ac(lambda e, h=h, bank=bank: e.activation(xnT[:, 4 + 512 * h:516 + 512 * h], bank[:, :], ACT.Identity, bias=lnb, scale=lng),
                       t, S["xnT"], l_v, c_z)
                PM.free(i, c)
                cp.append(c)
                for eb in range(2):
                    i, bank, w = PM.take()
                    t = pe(lambda e, h=h, eb=eb, bank=bank: e.matmul(bank[:, :], Win[:, 128 * eb:128 + 128 * eb],
                                                                    xnT[:, 4 + 512 * h:516 + 512 * h], start=True, stop=True), cp, l_win, w)
                    c = ac(lambda e, h=h, eb=eb, bank=bank: e.copy(zs[:, eb, 512 * h:512 * h + 512], bank[:, :]), t, S["zs"])
                    PM.free(i, c)
                    zz.append(c)
                for eb in range(2):
                    i, bank, w = PM.take()
                    for k in range(KC):
                        t = pe(lambda e, k=k, h=h, eb=eb, bank=bank: e.matmul(
                            bank[:, :], Wk[:, k, 128 * eb:128 * eb + 128], xnT[:, 1 + k + 512 * h:513 + k + 512 * h],
                            start=(k == 0), stop=(k == KC - 1)), c_wk, cp, w)
                    c = ac(lambda e, h=h, eb=eb, bank=bank: e.activation(u2[:, eb, 512 * h:512 * h + 512], bank[:, :], ACT.Identity,
                                                                        bias=cvb[:, eb:eb + 1]), t, S["u2"], l_v)
                    PM.free(i, c)
                    zz.append(c)
                    pr.append(t)
            G.free(il, *trs)

            def silus(e):
                done = [e.activation(v[:, :, :], v[:, :, :], ACT.Silu) for v in (zs, u2)]
                e.preload_act_table_set(TABLES)
                return 2600 + sum(done) if isinstance(done[0], float) else done[-1]

            uu = zz = [ac(silus, zz)]
            S["xnT"] = pr
            bc, dtd, dud = [], [], []
            for h in range(2):
                hs = slice(512 * h, 512 * h + 512)
                i, bank, w = PM.take()
                for eb in range(2):
                    t = pe(lambda e, eb=eb, hs=hs, bank=bank: e.matmul(bank[0:104, :], Wx[:, eb, :], u2[:, eb, hs],
                                                                      start=(eb == 0), stop=(eb == 1)), uu, wx, w)
                jr, rb, wr = G.take()
                Rs = rb[:, 0, :]
                hm_ = rb[:, 1, :].bitcast(BF16)
                Hs, Ms = hm_[0:96, 0:512], hm_[0:96, 512:1024]
                c0 = ac(lambda e, bank=bank, Rs=Rs: e.copy(Rs[96:104, :], bank[96:104, :]), t, wr)
                c1 = ac(lambda e, bank=bank, Hs=Hs: e.copy(Hs, bank[0:96, :]), t, wr)
                c2 = dv(lambda e, bank=bank, Rs=Rs, Hs=Hs: e.tensor_tensor(Rs[0:96, :], bank[0:96, :], Hs, ALU.subtract), c1)
                PM.free(i, c0, c2)
                c3 = dv(lambda e, Rs=Rs, Ms=Ms: e.tensor_copy(Ms, Rs[0:96, :]), c2)
                c4 = dv(lambda e, hs=hs, Rs=Rs, Ms=Ms: e.tensor_tensor(BC[64:96, hs], Rs[64:96, :], Ms[64:96, :], ALU.subtract), c3, S["BC"])
                c5 = ac(lambda e, hs=hs, Hs=Hs: e.copy(BC[0:32, hs], Hs[0:32, :]), c1, S["BC"])
                c6 = ac(lambda e, hs=hs, Ms=Ms: e.copy(BC[32:64, hs], Ms[32:64, :]), c3, S["BC"])
                bc += [c4, c5, c6]
                for eb in range(2):
                    i, bank, w = PM.take()
                    t = pe(lambda e, eb=eb, bank=bank, Rs=Rs: e.matmul(bank[:, :], Wdt[96:104, 128 * eb:128 * eb + 128], Rs[96:104, :],
                                                               start=True, stop=True), c0, l_wdt, w)
                    bb = bdt[:, eb:eb + 1]
                    ja, pa, wpa = dA.take()
                    jb, pb, wpb = G.take()
                    s0_, s1_, s2_, s3_ = pa[:, 0:1, :], pa[:, 1:2, :], pb[:, 0:1, :], pb[:, 1:2, :]
                    s0_, s1_, s2_, s3_ = (v.rearrange("p a n -> p (a n)") for v in (s0_, s1_, s2_, s3_))
                    d1 = ac(lambda e, s0_=s0_, s1_=s1_, s2_=s2_, s3_=s3_, bank=bank, bb=bb: e.activation(s0_, bank[:, :], ACT.Relu, bias=bb), t, wpa)
                    d2 = ac(lambda e, s0_=s0_, s1_=s1_, s2_=s2_, s3_=s3_, bank=bank, bb=bb: e.activation(s1_, bank[:, :], ACT.Abs, bias=bb), t, wpa)
                    PM.free(i, d1, d2)
                    d3 = ac(lambda e, s0_=s0_, s1_=s1_, s2_=s2_, s3_=s3_: e.activation(s1_, s1_, ACT.Exp, scale=-1.0), d2)
                    d4 = dv(lambda e, s0_=s0_, s1_=s1_, s2_=s2_, s3_=s3_: e.tensor_scalar(s2_, s1_, 1.0, -1.0, ALU.add, ALU.add), d3, wpb)
                    d5 = ac(lambda e, s0_=s0_, s1_=s1_, s2_=s2_, s3_=s3_: e.activation(s3_, s1_, ACT.Ln, bias=1.0), d3, wpb)
                    d6 = po(lambda e, s0_=s0_, s1_=s1_, s2_=s2_, s3_=s3_: e.tensor_tensor(s2_, s1_, s2_, ALU.subtract), d4)
                    d7 = po(lambda e, s0_=s0_, s1_=s1_, s2_=s2_, s3_=s3_: e.tensor_tensor(s3_, s3_, s2_, ALU.add), d5, d6)
                    d8 = po(lambda e, s0_=s0_, s1_=s1_, s2_=s2_, s3_=s3_, eb=eb, hs=hs: e.tensor_tensor(dtb[:, eb, hs], s3_, s0_, ALU.add), d7, d1, S["dt"])
                    d9 = po(lambda e, s0_=s0_, s1_=s1_, s2_=s2_, s3_=s3_, eb=eb, hs=hs: e.tensor_tensor(dtu[:, eb, hs], dtb[:, eb, hs], u2[:, eb, hs], ALU.mult), d8, uu)
                    dA.free(ja, d8)
                    G.free(jb, d8)
                    dtd.append(d8)
                    dud.append(d9)
                G.free(jr, t, c4, c5, c6)
            xs, alls = [], []
            for h in range(2):
                hs = slice(512 * h, 512 * h + 512)
                yt = [None, None]
                bch, dth, duh = bc[3 * h:3 * h + 3], dtd[2 * h:2 * h + 2], dud[2 * h:2 * h + 2]
                held = [PM.take() for _ in range(3)]
                Y, BB = [held[0][1], held[1][1]], held[2][1]
                ylast, S["bb"] = [held[0][2], held[1][2]], held[2][2]

                def broadcast(row, hs=hs, BB=BB):
                    t = pe(lambda e: e.matmul(BB[:, :], idm[:, row:row + 1].to_broadcast((96, 128)), BC[:, hs], start=True, stop=True),
                           bch, c_sel, S["bb"])
                    js, bs, wb = BS.take()
                    c = ac(lambda e: e.copy(bs[:, :], BB[:, :]), t, wb)
                    S["bb"] = [c]
                    return js, bs[:, :].unsqueeze(1).to_broadcast((128, 2, 512)), c

                def drive(n, hs=hs):
                    js, bs, c = broadcast(n)
                    ig, gb, wg = G.take()
                    v1 = (po if n % POOL == POOL - 1 else dv)(lambda e: e.tensor_tensor(gb[:, :, :], bs, dtu[:, :, hs], ALU.mult), c, duh, wg)
                    BS.free(js, v1)
                    S["dtu"].append(v1)
                    return ig, gb, v1

                if h == 0:
                    S["dtu"] = []
                driven = [drive(0)]
                for n in range(NS):
                    ig, gb, v1 = driven[n]
                    ia, da, wa = dA.take()
                    es = [ac(lambda e, eb=eb, n=n, da=da, hs=hs: e.activation(da[:, eb, :], dtb[:, eb, hs], ACT.Exp, scale=An[:, eb, n:n + 1]),
                             dth, c_an, wa) for eb in range(2)]
                    jc, cs, c = broadcast(16 + n)
                    if n + 1 < NS:
                        driven.append(drive(n + 1))
                    if n % 2 and n > 1:
                        add_up()
                    sc = [dv(lambda e, eb=eb, n=n, da=da, gb=gb, h=h: e.tensor_tensor_scan(
                        gb[:, eb, :], da[:, eb, :], gb[:, eb, :], 0.0 if h == 0 else hl[:, eb, n:n + 1], ALU.mult, ALU.add),
                        es[eb], v1, S["hl"] if h else None) for eb in range(2)]
                    dA.free(ia, *sc)
                    v3 = None
                    if h == 0:
                        v3 = dv(lambda e, n=n, gb=gb: e.tensor_copy(hl[:, :, n:n + 1], gb[:, :, 511:512]), sc, S["hl"], c_z)
                        alls.append(v3)
                    v2 = dv(lambda e, gb=gb, cs=cs: e.tensor_tensor(gb[:, :, :], cs, gb[:, :, :], ALU.mult), c, sc, v3)
                    BS.free(jc, v2)

                    if n % 2 == 0:
                        ie, ge, even = ig, gb, v2
                        continue
                    ad = po(lambda e, gb=gb, ge=ge: e.tensor_tensor(gb[:, :, :], ge[:, :, :], gb[:, :, :], ALU.add), even, v2)
                    G.free(ie, ad)

                    def add_up(n=n, ig=ig, gb=gb, ad=ad, Y=Y):
                        for eb in range(2):
                            yt[eb] = pe(lambda e, eb=eb: e.matmul(Y[eb][:, :], ident, gb[:, eb, :], start=(n == 1), stop=(n == NS - 1)),
                                        ad, ylast)
                        G.free(ig, yt[1])
                add_up()
                if h == 0:
                    S["hl"] = alls
                jy, yg, wy = G.take()
                ys = [dv(lambda e, eb=eb, hs=hs, yg=yg, Y=Y: e.scalar_tensor_tensor(yg[:, eb, :], u2[:, eb, hs], Dp[:, eb:eb + 1], Y[eb][:, :],
                                                                              ALU.mult, ALU.add), yt[1], wy, l_v) for eb in range(2)]
                for k, x in ((0, ys[0]), (1, ys[1]), (2, S["bb"][0])):
                    PM.free(held[k][0], x)
                gt = po(lambda e, hs=hs, yg=yg: e.tensor_tensor(yg[:, :, :], yg[:, :, :], zs[:, :, hs], ALU.mult), ys, zz)
                i, bank, w = PM.take()
                for k in range(4):
                    for eb in range(2):
                        t = pe(lambda e, k=k, eb=eb, bank=bank, yg=yg: e.matmul(
                            bank[:, 128 * k:128 * k + 128], yg[:, eb, 128 * k:128 * k + 128],
                            Wout[:, eb, :], start=(eb == 0), stop=(eb == 1)), gt, l_wo, w)
                G.free(jy, t)
                xv = X[:, 8 * b + 4 * h:8 * b + 4 * h + 4, :].rearrange("p a c -> p (a c)")
                x1 = dv(lambda e, xv=xv, bank=bank, h=h: e.scalar_tensor_tensor(
                    xv, bank[:, :], res, xv, ALU.mult, ALU.add), t, xa, l_res)
                PM.free(i, x1)
                xs.append(x1)
            S["zs"] = [gt]
            S["u2"] = [gt] + ys
            S["dt"] = sc + S["dtu"]
            S["BC"] = S["bb"]
            S["hl"] = sc
            xready[b] = [xs[k // 4] for k in range(8)]

        outs = []

        def store(b):
            q.stream("ffn")
            outs.append(dma(lambda e: e.dma_start(out[b].rearrange("(i p) c -> p i c", p=128), X[:, 8 * b:8 * b + 8, :]), xready[b]))

        later = PA, PF
        PA, PF = Slots(banks[0:3] + banks[5:8]), Slots(banks[3:5])
        attention(0)
        ffn(0)
        PA, PF = later
        for b in range(NB):
            if b + 1 < NB:
                attention(b + 1)
                ffn(b + 1)
            if b > 0:
                ffn(b - 1)
                store(b - 1)
            mamba(b)
        ffn(NB - 1)
        store(NB - 1)
        q.merge()

        sems = {e: ctx.enter_context(nc.semaphore(f"s_{e}")) for e in Queue.ENGINES}
        count = [0]

        def new_sem():
            count[0] += 1
            return ctx.enter_context(nc.semaphore(f"s_dma{count[0]}"))

        q.number(sems, new_sem)
        block = ctx.enter_context(nc.Block())

        @block.sync
        def _(eng):
            q.write("sync", eng)
            for t in outs:
                eng.wait_ge(t.sem, 16)

        @block.tensor
        def _(eng):
            q.write("tensor", eng)

        @block.vector
        def _(eng):
            q.write("vector", eng)

        @block.scalar
        def _(eng):
            q.write("scalar", eng)

        @block.gpsimd
        def _(eng):
            q.write("gpsimd", eng)


STAGES = ("mamba", "attention", "ffn")
STREAMS = ("attention", "heads0", "heads1", "heads2", "mamba", "join", "prepare", "ffn")

_INS = {"x": "L0_attn_a_x", "Wq": "L0_attn_a_Wq", "Wk": "L0_attn_a_Wk", "Wv": "L0_attn_a_Wv", "Wo": "L0_attn_a_Wo",
        "ln_g": "L0_attn_b_ln_g", "ln_b": "L0_attn_b_ln_b", "W_in": "L0_attn_b_W_in", "conv_w": "L0_attn_b_conv_w",
        "conv_b": "L0_attn_b_conv_b", "W_xp": "L0_attn_b_W_xp", "W_dt": "L0_attn_b_W_dt", "b_dt": "L0_attn_b_b_dt",
        "A_log": "L0_attn_b_A_log", "D_param": "L0_attn_b_D_param", "W_out": "L0_attn_b_W_out", "res": "L0_attn_b_res_scale",
        "k0": "L0_ffn_k0", "k1": "L0_ffn_k1", "k2": "L0_ffn_k2", "s0": "L0_ffn_s0", "s1": "L0_ffn_s1", "s2": "L0_ffn_s2"}


def kernel(**inputs):
    import numpy as _np
    import concourse.bacc as _bacc
    from concourse import mybir as _mybir
    from concourse.bass_utils import run_bass_kernel_spmd as _run

    nc = _bacc.Bacc("TRN2", target_bir_lowering=False, num_devices=1)
    arrays, args = {}, {}
    for short, name in _INS.items():
        a = _np.ascontiguousarray(inputs[name])
        if short in ("s0", "s1", "s2", "res"):
            a = a.reshape(1, 1)
        arrays[f"in_{short}"] = a
        args[short] = nc.dram_tensor(f"in_{short}", a.shape, _mybir.dt.from_np(a.dtype), kind="ExternalInput").ap()
    c = constants()
    arrays["in_consts"] = c
    args["consts"] = nc.dram_tensor("in_consts", c.shape, _mybir.dt.from_np(c.dtype), kind="ExternalInput").ap()
    o = nc.dram_tensor("out_0", (NB, T, C), _mybir.dt.float32, kind="ExternalOutput").ap()
    hybrid_block(nc, args, o)
    r = _run(nc, [arrays], core_ids=[0])
    return r.results[0]["out_0"]
```
